# Optimizing a Trainium2 kernel written in Bass

```python
import numpy as np
import jax
import jax.numpy as jnp

def _softmax(x, axis=-1):
    return jax.nn.softmax(x, axis=axis)

def _gelu(x):
    return jax.nn.gelu(x, approximate=True)

def _silu(x):
    return jax.nn.silu(x)

def _sigmoid(x):
    return jax.nn.sigmoid(x)

def _layernorm(x, axis=-1, eps=1e-05):
    m = jnp.mean(x, axis=axis, keepdims=True)
    v = jnp.var(x, axis=axis, keepdims=True)
    return (x - m) / jnp.sqrt(v + eps)

def _scatter_add(tgt, idx, src, axis=0):
    return tgt.at[idx].add(src)

def _segment_sum(src, seg, n):
    return jax.ops.segment_sum(src, seg, n)
kernel_name = 'mk_seq_preln_d1_jaxref_r4_56402a'

def setup_inputs(seed: int=0):
    np.random.seed(seed)
    _w = jnp.asarray

    def _L0_attn_setup():
        import jax, jax.numpy as jnp
        import numpy as np
        EMBED_DIM = 512
        NUM_HEADS = 32
        HEAD_DIM = EMBED_DIM // NUM_HEADS
        BATCH = 2
        SEQ_LEN = 512
        key = jax.random.key(seed)
        ks = jax.random.split(key, 5)
        scale = 1.0 / np.sqrt(EMBED_DIM)
        x = jax.random.normal(ks[0], (BATCH, SEQ_LEN, EMBED_DIM), dtype=jnp.float32)
        Wq = jax.random.normal(ks[1], (EMBED_DIM, EMBED_DIM), dtype=jnp.float32) * scale
        Wk = jax.random.normal(ks[2], (EMBED_DIM, EMBED_DIM), dtype=jnp.float32) * scale
        Wv = jax.random.normal(ks[3], (EMBED_DIM, EMBED_DIM), dtype=jnp.float32) * scale
        Wo = jax.random.normal(ks[4], (EMBED_DIM, EMBED_DIM), dtype=jnp.float32) * scale
        return {'x': x, 'Wq': Wq, 'Wk': Wk, 'Wv': Wv, 'Wo': Wo}
    _L0_attn_in = _L0_attn_setup()

    def _L0_ffn_setup():
        import jax, jax.numpy as jnp
        import numpy as np
        HIDDEN = 512
        INTER = 1376
        LUT_SIZE = 16

        def _ghost_linear(x, idx, lut):
            w = lut[idx]
            return jnp.einsum('bsh,oh->bso', x, w)
        key = jax.random.key(seed)
        k_x, k_lut, k_g, k_u, k_d = jax.random.split(key, 5)
        x = jax.random.normal(k_x, (2, 1024, HIDDEN), dtype=jnp.float32)
        lut = jax.random.normal(k_lut, (LUT_SIZE,), dtype=jnp.float32) * 0.02
        gate_idx = jax.random.randint(k_g, (INTER, HIDDEN), 0, LUT_SIZE, dtype=jnp.int32)
        up_idx = jax.random.randint(k_u, (INTER, HIDDEN), 0, LUT_SIZE, dtype=jnp.int32)
        down_idx = jax.random.randint(k_d, (HIDDEN, INTER), 0, LUT_SIZE, dtype=jnp.int32)
        return {'x': x, 'lut': lut, 'gate_idx': gate_idx, 'up_idx': up_idx, 'down_idx': down_idx}
    _L0_ffn_in = _L0_ffn_setup()
    _d = {'L0_attn_x': _L0_attn_in['x'], 'L0_attn_Wq': _L0_attn_in['Wq'], 'L0_attn_Wk': _L0_attn_in['Wk'], 'L0_attn_Wv': _L0_attn_in['Wv'], 'L0_attn_Wo': _L0_attn_in['Wo'], 'L0_ffn_lut': _L0_ffn_in['lut'], 'L0_ffn_gate_idx': _L0_ffn_in['gate_idx'], 'L0_ffn_up_idx': _L0_ffn_in['up_idx'], 'L0_ffn_down_idx': _L0_ffn_in['down_idx']}
    _x0 = _d['L0_attn_x']
    _d['L0_attn_x'] = jax.random.normal(jax.random.fold_in(jax.random.key(seed), 1), (2, 2048, 512), dtype=_x0.dtype)
    del _x0
    return _d

def reference(L0_attn_x, L0_attn_Wq, L0_attn_Wk, L0_attn_Wv, L0_attn_Wo, L0_ffn_lut, L0_ffn_gate_idx, L0_ffn_up_idx, L0_ffn_down_idx):

    def _L0_attn_ref(x, Wq, Wk, Wv, Wo):
        import jax, jax.numpy as jnp
        import numpy as np
        EMBED_DIM = 512
        NUM_HEADS = 32
        HEAD_DIM = EMBED_DIM // NUM_HEADS
        BATCH = 2
        SEQ_LEN = 512
        q = jnp.einsum('bse,ef->bsf', x, Wq)
        k = jnp.einsum('bse,ef->bsf', x, Wk)
        v = jnp.einsum('bse,ef->bsf', x, Wv)
        qT = jnp.swapaxes(q, 1, 2)
        kT = jnp.swapaxes(k, 1, 2)
        vT = jnp.swapaxes(v, 1, 2)
        attn_scores = jnp.einsum('bes,bfs->bef', qT, kT) / np.sqrt(HEAD_DIM)
        attn_weights = jax.nn.softmax(attn_scores, axis=-1)
        attn_output = jnp.einsum('bef,bfs->bes', attn_weights, vT)
        attn_output = jnp.swapaxes(attn_output, 1, 2)
        return jnp.einsum('bse,ef->bsf', attn_output, Wo)

    def _L0_ffn_ref(x, lut, gate_idx, up_idx, down_idx):
        import jax, jax.numpy as jnp
        import numpy as np
        HIDDEN = 512
        INTER = 1376
        LUT_SIZE = 16

        def _ghost_linear(x, idx, lut):
            w = lut[idx]
            return jnp.einsum('bsh,oh->bso', x, w)
        gate = _ghost_linear(x, gate_idx, lut)
        up = _ghost_linear(x, up_idx, lut)
        h = jax.nn.silu(gate) * up
        return _ghost_linear(h, down_idx, lut)
    x = L0_attn_x
    x = x + _L0_attn_ref(_layernorm(x, axis=-1), L0_attn_Wq, L0_attn_Wk, L0_attn_Wv, L0_attn_Wo)
    x = x + _L0_ffn_ref(_layernorm(x, axis=-1), L0_ffn_lut, L0_ffn_gate_idx, L0_ffn_up_idx, L0_ffn_down_idx)
    return x

_drawn_inputs = setup_inputs


def setup_inputs(seed=0):
    import zlib

    import numpy as np

    out = dict(_drawn_inputs(seed))
    spreads = {}
    factors = {}
    for name, (base, spread) in spreads.items():
        noise = np.random.default_rng([zlib.crc32(name.encode()), seed]).standard_normal(out[name].shape)
        drawn = base * np.exp(spread * noise) if base else spread * noise
        out[name] = jnp.asarray(drawn.astype(out[name].dtype))
    for name, factor in factors.items():
        out[name] = (out[name] * factor).astype(out[name].dtype)
    return out
```

```python
from contextlib import ExitStack

import concourse.bass as bass
from concourse import mybir
from concourse.alu_op_type import AluOpType as ALU

ACT = mybir.ActivationFunctionType
AX_X = mybir.AxisListType.X
F32 = mybir.dt.float32
F32R = mybir.dt.float32r
BF16 = mybir.dt.bfloat16
I32 = mybir.dt.int32
I16 = mybir.dt.int16

P = 128
EPS = 1e-5
RSQRT_SEED = float(0x5F3759DF)
NEWTON = 3
KIB = 1024


def preln_attention_ghost_ffn(nc, x_in, wq_in, wk_in, wv_in, wo_in, lut_in, gate_in, up_in, down_in, out):
    B, S, D = x_in.shape
    I = gate_in.shape[0]
    LUT = lut_in.shape[0]
    K = D // P
    T = 4
    BT = T * P
    NG = B * S // BT
    GB = S // BT
    C = -(-I // P)
    HALF = LUT // 2
    SCALE = 1.0 / float((D // 32) ** 0.5)

    def rows(c):
        return min(P, I - c * P)

    U = 3 * C
    U_IDX_EARLY = 15
    U_EARLY = 21
    assert (D, K, C, NG, GB, LUT) == (512, 4, 11, 8, 4, 16)

    xb_dram = x_in.rearrange("b s d -> (b s) d").rearrange("(n p t) d -> n p t d", p=P, t=T)
    ob_dram = out.rearrange("b s d -> (b s) d").rearrange("(n p t) d -> n p t d", p=P, t=T)

    ctx = ExitStack()
    with ctx:
        base = 16512

        def at(name, kib, shape, dt):
            return nc.alloc_sbuf_tensor_at(name, shape, dt, offset=base + int(kib * KIB))

        def sem(name):
            return ctx.enter_context(nc.semaphore(name))

        w_hi = [at(f"w_hi{c}", 12 * c, [P, 3, D], F32R) for c in range(C)]
        w_lo = [at(f"w_lo{c}", 12 * c + 6, [P, 3, D], F32R) for c in range(C)]
        idx_t = [at(f"idx_t{c}", 12 * c + 9, [P, 3, D], I16) for c in range(C)]
        x2t_hi = at("x2t_hi", 132, [P, K, BT], F32R)
        x2t_lo = at("x2t_lo", 140, [P, K, BT], F32R)
        m_hi = at("m_hi", 148, [P, K, D], F32R)
        m_lo = at("m_lo", 156, [P, K, D], F32R)
        x1 = [at("x1a", 164, [P, T, D], F32), at("x1b", 188, [P, T, D], F32)]
        h_hi = [at(f"h_hi{i}", 172 + 4 * i, [P, BT], F32R) for i in range(2)]
        h_lo = [at(f"h_lo{i}", 174 + 4 * i, [P, BT], F32R) for i in range(2)]
        h_gate = at("h_gate", 180, [P, BT], F32)
        h_full = at("h_full", 182, [P, BT], F32)
        xt_hi = at("xt_hi", 184, [P, K, P], F32R)
        xt_lo = at("xt_lo", 186, [P, K, P], F32R)
        xn = at("xn", 196, [P, T, D], F32)
        xn_first = at("xn_first", 172, [P, T, D], F32)
        mat_x = [(at(f"mat_x_hi{b}", 60 + 32 * b, [P, K, D], F32R), at(f"mat_x_lo{b}", 68 + 32 * b, [P, K, D], F32R)) for b in range(B)]
        mat_y = [(at(f"mat_y_hi{b}", 76 + 32 * b, [P, K, D], F32R), at(f"mat_y_lo{b}", 84 + 32 * b, [P, K, D], F32R)) for b in range(B)]
        wa = (at("wa_hi", 132, [P, K, D], F32R), at("wa_lo", 140, [P, K, D], F32R))
        wb = (at("wb_hi", 164, [P, K, D], F32R), at("wb_lo", 124, [P, K, D], F32R))
        raw = [at(f"raw{i}", 184 + 2 * i, [P, D], F32) for i in range(2)]
        full = [at(f"full{i}", 178 + 2 * i, [P, D], F32) for i in range(2)]
        xg = [at(f"xg{i}", 76 + 8 * i, [P, T, D], F32) for i in range(2)]
        xg_hi = [at(f"xg_hi{i}", 108 + 4 * i, [P, D], F32R) for i in range(4)]
        xg_lo = [at(f"xg_lo{i}", 110 + 4 * i, [P, D], F32R) for i in range(4)]
        xg_n = [at(f"xg_n{i}", 148 + 2 * i, [P, D], F32) for i in range(4)]
        idx_raw = [at(f"idx_raw{i}", 172 + 2 * i, [P, D], I32) for i in range(2)]
        idx_bf = [at(f"idx_bf{i}", 176 + 1 * i, [P, D], BF16) for i in range(2)]
        picked = [at("picked0", 188, [P, D], F32), at("picked1", 190, [P, D], F32)]
        part = [at(f"part{i}", kib, [P, D], F32) for i, kib in enumerate((192, 194, 196, 205.75))]
        high_mask = at("high_mask", 198, [P, D], I32)
        bit_mask = [at(f"bit_mask{i}", 200 + i, [P, D], I16) for i in range(3)]
        ident = at("ident", 204, [P, P], F32)
        ident_bf = at("ident_bf", 204.5, [P, P], BF16)
        lut = at("lut", 204.75, [P, LUT], F32)
        lut_x = at("lut_x", 204.8125, [P, HALF], I32)
        bn = at("bn", 204.875, [P, T, 6], F32)
        mv = at("mv", 205, [P, T, 2], F32)
        var = at("var", 205.0625, [P, T], F32)
        tmp = at("tmp", 205.125, [P, T], F32)
        rstd = [at(f"rstd{i}", 205.1875 + i / 16, [P, T], F32) for i in range(2)]
        shift = [at(f"shift{i}", 205.3125 + i / 16, [P, T], F32) for i in range(2)]
        smax = at("smax", 205.4375, [P, 2 * K], F32)
        sbias = at("sbias", 205.5, [P, 2 * K], F32)
        ssum = at("ssum", 205.5625, [P, 2 * K], F32)
        srec = at("srec", 205.625, [P, 2 * K], F32)

        bank = [ctx.enter_context(nc.psum_tensor(f"bank{i}", [P, D], F32)) for i in range(8)]
        m_dram = nc.dram_tensor("m_scratch", (B, 2, P, K * D), F32).ap()

        const_made = sem("const_made")
        lut_loaded = sem("lut_loaded")
        dve_steps = sem("dve_steps")
        idx_loaded = [sem(f"idx_loaded{i}") for i in range(2)]
        idx_cast = sem("idx_cast")
        idx_turned = sem("idx_turned")
        idx_laid = sem("idx_laid")
        picked_done = sem("picked_done")
        w_hi_done = sem("w_hi_done")
        w_lo_done = sem("w_lo_done")
        xg_loaded = [sem(f"xg_loaded{i}") for i in range(2)]
        xg_stats = sem("xg_stats")
        xg_normed = sem("xg_normed")
        xg_hi_done = sem("xg_hi_done")
        xg_lo_done = sem("xg_lo_done")
        xg_used = sem("xg_used")
        raw_loaded = [sem(f"raw_loaded{i}") for i in range(2)]
        raw_hi_done = sem("raw_hi_done")
        raw_lo_done = sem("raw_lo_done")
        product_done = sem("product_done")
        product_taken = sem("product_taken")
        product_hi = sem("product_hi")
        product_lo = sem("product_lo")
        smax_done = sem("smax_done")
        sbias_done = sem("sbias_done")
        sexp_done = sem("sexp_done")
        srec_done = sem("srec_done")
        snorm_done = sem("snorm_done")
        m_stored = sem("m_stored")
        m_loaded = sem("m_loaded")
        x_loaded = [sem(f"x_loaded{i}") for i in range(2)]
        out_stored = [sem(f"out_stored{i}") for i in range(2)]
        ln1_stats = sem("ln1_stats")
        ln1_done = sem("ln1_done")
        xt_turned = sem("xt_turned")
        xt_hi_done = sem("xt_hi_done")
        xt_lo_done = sem("xt_lo_done")
        attn_done = sem("attn_done")
        x1_done = sem("x1_done")
        ln2_stats = sem("ln2_stats")
        ln2_done = sem("ln2_done")
        x2_turned = sem("x2_turned")
        x2_hi_done = sem("x2_hi_done")
        x2_lo_done = sem("x2_lo_done")
        gate_done = sem("gate_done")
        up_done = sem("up_done")
        silu_done = sem("silu_done")
        h_done = sem("h_done")
        h_hi_done = sem("h_hi_done")
        h_lo_done = sem("h_lo_done")
        down_done = sem("down_done")
        y_added = sem("y_added")

        GRAM, PROD, SCORE, TURN_V, MIX, FOLD = "gram", "prod", "score", "turn_v", "mix", "fold"
        groups = [(GRAM, 0), (GRAM, 1), (PROD, 0), (PROD, 1), (SCORE, 0), (SCORE, 1),
                  (TURN_V, 0), (MIX, 0), (MIX, 1), (FOLD, 0), (FOLD, 1)]
        number = {g: q for q, g in enumerate(groups)}
        LAST_ITEM = K * len(groups)
        WK, WQ, WO, WV = range(4)
        raws = [wk_in, wq_in, wo_in, wv_in]
        split_into = {WK: wa, WQ: wb, WO: wa}

        def product_bank(n):
            return bank[4 * (n // K % 2) + n % K]

        def result_of(n):
            (name, b), m = groups[n // K], n % K
            if name == TURN_V:
                return [a[:, :, m * P:(m + 1) * P] for a in wb]
            pair = {GRAM: mat_x[b], SCORE: mat_x[b], PROD: mat_y[b], MIX: mat_y[b],
                    FOLD: (m_hi, m_lo) if b == 0 else mat_x[1]}[name]
            return [a[:, m, :] for a in pair]

        def as_result(n, tile):
            return tile[:].rearrange("p (k d) -> p k d", k=K) if groups[n // K][0] == TURN_V else tile[:]

        def is_score(n):
            return groups[n // K][0] == SCORE

        timeline = []
        quarters = iter([(u, q) for u in range(U_IDX_EARLY) for q in range(4)])

        def build(n):
            timeline.extend(("build", x) for _, x in zip(range(n), quarters))

        for g in range(NG):
            if g < U_IDX_EARLY // 3:
                timeline += [("idx", u) for u in range(3 * g, 3 * g + 3)]
            timeline.append(("gram", g))
            if 3 <= g < 7:
                w, k0 = divmod(2 * (g - 3), K)
                timeline += [("raw", (w, k0)), ("raw", (w, k0 + 1))]
            if g == GB:
                timeline += [("take", n) for n in range(K)]
            build(2 if g else 0)
        for n in range(K, LAST_ITEM):
            if n >= 2 * K:
                timeline.append(("product", n))
            timeline.append(("take", n))
            if is_score(n):
                if is_score(n - 1):
                    timeline.append(("norm", n - 1))
                if not is_score(n + 1):
                    timeline.append(("norm", n))
                if n < K * (number[(SCORE, 0)] + 1):
                    timeline.append(("raw", (WO, n % K)))
            build(1 + (n % 5 == 0))
        build(4 * U)
        quarters = iter([(u, q) for u in range(U_IDX_EARLY, U_EARLY) for q in range(4)])
        for i in range(3):
            n_idx = (U - U_IDX_EARLY) // 3
            timeline += [("idx", U_IDX_EARLY + n_idx * i + x) for x in range(n_idx)]
            build(4)
        timeline.append(("first", "ln1"))
        build(2)
        for t in range(T):
            timeline.append(("first", t))
            build(2)
        timeline.append(("first", "ln2"))
        build(4 * U)
        timeline.append(("first", "x2"))

        def late_units(c):
            return [u for u in range(U_EARLY, U) if (u - U_EARLY) * 9 // (U - U_EARLY) == c]

        class Block:

            def __init__(self, j, off):
                self.j, self.off = j, off
                fixed = isinstance(j, int)
                self.n = 2 * j + off
                self.first = fixed and self.n == 0
                self.last = fixed and self.n == NG - 1
                self.parity = off % 2
                self.half = j + off // 2

            def next(self):
                return None if self.last else Block(self.j, self.off + 1)

            def count(self, per, i):
                return per * self.n + (i + 1)

        LN1_STATS, LN1, TURN, LN2 = 1, 2, 3, 8

        def preparation(b, c):
            if b.last:
                return []
            if b.first:
                every = ["stats1", "ln1", ("turn", 0)]
                for t in range(T):
                    every += [("attend", t)] + ([("turn", t + 1)] if t + 1 < T else [])
                return every + ["stats2", "ln2"] if c == C - 1 else []
            steps = {LN1_STATS: ["stats1"], LN1: ["ln1"], LN2: ["ln2"], TURN + T: [("attend", T - 1), "stats2"]}
            for t in range(T):
                if TURN + t <= c and c == TURN + t:
                    return ([("attend", t - 1)] if t else []) + [("turn", t)]
            return steps.get(c, [])

        def every_block(eng, run):
            with eng.Fori(0, (NG - 2) // 2) as j:
                run(Block(j, 1))
                run(Block(j, 2))
            run(Block(0, NG - 1))

        blk = ctx.enter_context(nc.Block())

        @blk.sync
        def _(sp):
            def load_idx(u):
                c, kind = u // 3, u % 3
                if u >= 2:
                    sp.wait_ge(idx_cast, u - 1)
                n = rows(c)
                if kind < 2:
                    src = (gate_in, up_in)[kind][c * P:c * P + n, :]
                    sp.dma_start(idx_raw[u % 2][0:n, :], src).then_inc(idx_loaded[u % 2], 16)
                else:
                    src = down_in[:, c * P:c * P + n].rearrange("(k p) i -> p k i", p=P)
                    dst = idx_raw[u % 2][:, :].rearrange("p (k i) -> p k i", k=K)[:, :, 0:n]
                    sp.dma_start(dst, src).then_inc(idx_loaded[u % 2], 16)

            def load_raw(w, k):
                r = K * w + k
                if r >= K * WV + 2:
                    sp.wait_ge(product_done, K * number[(TURN_V, 0)] + r - K * WV - 1)
                elif r >= 2:
                    sp.wait_ge(raw_lo_done, r - 1)
                sp.dma_start(raw[r % 2][:], raws[w][k * P:(k + 1) * P, :]).then_inc(raw_loaded[r % 2], 16)

            sp.dma_start(xg[0][:], xb_dram[0]).then_inc(xg_loaded[0], 16)
            for stage, arg in timeline:
                if stage == "idx" and arg < U_IDX_EARLY:
                    load_idx(arg)
                if stage == "gram" and arg + 1 < NG:
                    if arg >= 1:
                        sp.wait_ge(xg_normed, T * arg)
                    sp.dma_start(xg[(arg + 1) % 2][:], xb_dram[arg + 1]).then_inc(xg_loaded[(arg + 1) % 2], 16)
                if stage == "raw":
                    load_raw(*arg)
            load_raw(WV, 0)
            load_raw(WV, 1)
            load_idx(U_IDX_EARLY)
            load_idx(U_IDX_EARLY + 1)
            load_raw(WV, 2)
            load_raw(WV, 3)

            def flat(tile):
                return tile[:].rearrange("p k d -> p (k d)").bitcast(F32)

            for b, pair in enumerate(((m_hi, m_lo), mat_x[1])):
                sp.wait_ge(product_lo, K * (number[(FOLD, b)] + 1))
                for i in range(2):
                    sp.dma_start(m_dram[b, i], flat(pair[i])).then_inc(m_stored, 16)

            def load_x(b):
                sp.dma_start(x1[b.parity][:], xb_dram[b.n]).then_inc(x_loaded[b.parity], 16)

            def store(b):
                sp.wait_ge(y_added, b.count(T, T - 1))
                sp.dma_start(ob_dram[b.n], x1[b.parity][:]).then_inc(out_stored[b.parity], 16)

            def reload_x(b):
                sp.wait_ge(out_stored[b.parity], 16 * b.half)
                load_x(b)

            def load_m(b):
                sp.wait_ge(attn_done, T * b.n)
                for i, half in enumerate((m_hi, m_lo)):
                    sp.dma_start(flat(half), m_dram[b.half // (GB // 2), i]).then_inc(m_loaded, 16)

            load_x(Block(0, 0))
            for u in range(U_IDX_EARLY + 2, U):
                load_idx(u)
            sp.wait_ge(w_lo_done, U)
            load_x(Block(0, 1))
            sp.wait_ge(m_stored, 16 * 2 * B)
            store(Block(0, 0))
            reload_x(Block(0, 2))
            with sp.Fori(0, (NG - 4) // 2) as j:
                load_m(Block(j, 2))
                store(Block(j, 1))
                reload_x(Block(j, 3))
                store(Block(j, 2))
                reload_x(Block(j, 4))
            load_m(Block(0, NG - 2))
            store(Block(0, NG - 3))
            reload_x(Block(0, NG - 1))
            store(Block(0, NG - 2))
            store(Block(0, NG - 1))
            for i in range(2):
                sp.wait_ge(out_stored[i], 16 * (NG // 2))

        @blk.gpsimd
        def _(pool):
            pool.dma_start(lut[:], lut_in.rearrange("(a n) -> a n", a=1).to_broadcast([P, LUT])).then_inc(lut_loaded, 16)
            pool.memset(ident[:], 0.0).then_inc(const_made, 1)
            pool.memset(ident_bf[:], 0.0).then_inc(const_made, 1)
            pool.wait_ge(const_made, 2)
            for one in (ident, ident_bf):
                pool.affine_select(out=one[:], in_=one[:], compare_op=ALU.not_equal, fill=1.0, base=0,
                                   pattern=[[-1, P]], channel_multiplier=1).then_inc(const_made, 1)

            def low(out_, whole, high):
                return pool.tensor_tensor(out_, whole, high.bitcast(F32), ALU.subtract)

            def weight_low(u):
                c, kind = u // 3, u % 3
                pool.wait_ge(w_hi_done, u + 1)
                low(w_lo[c][:, kind, :], picked[u % 2][:], w_hi[c][:, kind, :]).then_inc(w_lo_done, 1)

            for stage, arg in timeline:
                if stage == "idx" and arg == U_IDX_EARLY:
                    pool.wait_ge(m_stored, 16 * 2 * B)
                    pool.memset(idx_t[C - 1][:], 0).then_inc(const_made, 1)
                if stage == "gram":
                    for i in range(T * arg, T * arg + T):
                        pool.wait_ge(xg_hi_done, i + 1)
                        low(xg_lo[i % 4][:], xg_n[i % 4][:], xg_hi[i % 4][:]).then_inc(xg_lo_done, 1)
                if stage == "raw":
                    w, k = arg
                    r = K * w + k
                    pool.wait_ge(raw_hi_done, r + 1)
                    hi, lo = split_into[w]
                    low(lo[:, k, :], raw[r % 2][:], hi[:, k, :]).then_inc(raw_lo_done, 1)
                if (stage == "take" and not is_score(arg)) or stage == "norm":
                    hi, lo = result_of(arg)
                    pool.wait_ge(product_hi, arg + 1)
                    pool.wait_ge(product_taken, arg + 1)
                    low(lo, as_result(arg, full[arg % 2]), hi).then_inc(product_lo, 1)
                if stage == "build" and arg[1] == 3:
                    weight_low(arg[0])

            def ffn(b):
                for c in range(C):
                    n = rows(c)
                    pool.wait_ge(h_hi_done, b.count(C, c))
                    low(h_lo[c % 2][0:n, :], h_full[0:n, :], h_hi[c % 2][0:n, :]).then_inc(h_lo_done, 1)
                    if b.first:
                        for u in late_units(c):
                            weight_low(u)

            ffn(Block(0, 0))
            every_block(pool, ffn)

        @blk.scalar
        def _(act):
            def weight_high(u):
                c, kind = u // 3, u % 3
                act.wait_ge(picked_done, u + 1)
                act.copy(w_hi[c][:, kind, :], picked[u % 2][:]).then_inc(w_hi_done, 1)

            def turn_first(step):
                if step == "ln1":
                    act.wait_ge(product_lo, LAST_ITEM)
                    act.wait_ge(idx_turned, U)
                    normalise(Block(0, 0), xn_first, 0)
                elif step == "ln2":
                    normalise(Block(0, 0), xn_first, 1)
                elif step == "x2":
                    x2_high(Block(0, 0))
                else:
                    x_high(Block(0, 0), step)

            def normalise(b, into, second):
                stats, done = ((ln1_stats, ln1_done), (ln2_stats, ln2_done))[second]
                act.wait_ge(stats, b.count(1, 0))
                for t in range(T):
                    act.activation(into[:, t, :], x1[b.parity][:, t, :], ACT.Identity, bias=shift[second][:, t:t + 1],
                                   scale=rstd[second][:, t:t + 1]).then_inc(done, 1)

            def x_high(b, t):
                act.wait_ge(xt_turned, b.count(T, t))
                if not (b.first and t == 0):
                    act.wait_ge(attn_done, b.count(T, t - 1))
                else:
                    act.wait_ge(product_done, K * (number[(TURN_V, 0)] + 1))
                act.copy(xt_hi[:].rearrange("p k s -> p (k s)"), bank[6][:]).then_inc(xt_hi_done, 1)

            def x2_high(b):
                for k in range(K):
                    act.wait_ge(x2_turned, b.count(K, k))
                    act.copy(x2t_hi[:, k, :], bank[6 + k % 2][:]).then_inc(x2_hi_done, 1)

            for stage, arg in timeline:
                if stage == "idx":
                    u, c, kind = arg, arg // 3, arg % 3
                    n = rows(c)
                    act.wait_ge(idx_loaded[u % 2], 16 * (u // 2 + 1))
                    if u >= 2:
                        act.wait_ge(idx_turned, u - 1)
                    src, dst = idx_raw[u % 2][:, :], idx_bf[u % 2][:, :]
                    if kind < 2:
                        src, dst = src[0:n, :], dst[0:n, :]
                    else:
                        src, dst = (a.rearrange("p (k i) -> p k i", k=K)[:, :, 0:n] for a in (src, dst))
                    act.copy(dst, src).then_inc(idx_cast, 1)
                    act.wait_ge(idx_turned, u + 1)
                    if u == U_IDX_EARLY:
                        act.wait_ge(m_stored, 16 * 2 * B)
                        act.wait_ge(const_made, 5)
                    src = bank[4 + u % 4][:].bitcast(BF16)[:, 0:D].rearrange("p (k i) -> p k i", k=K)
                    dst = idx_t[c][:, kind, :].rearrange("p (k i) -> p k i", k=K)
                    if kind < 2:
                        src, dst = src[:, :, 0:n], dst[:, :, 0:n]
                    else:
                        src, dst = src[0:n], dst[0:n]
                    act.copy(dst, src).then_inc(idx_laid, 1)
                if stage == "gram":
                    g = arg
                    act.wait_ge(xg_stats, g + 1)

                    def high(i):
                        act.wait_ge(xg_normed, i + 1)
                        if i >= 4:
                            act.wait_ge(xg_used, i - 3)
                        act.copy(xg_hi[i % 4][:], xg_n[i % 4][:]).then_inc(xg_hi_done, 1)

                    for t in range(T):
                        i = T * g + t
                        if i >= 4:
                            act.wait_ge(xg_lo_done, i - 3)
                        act.activation(xg_n[i % 4][:], xg[g % 2][:, t, :], ACT.Identity, bias=shift[g % 2][:, t:t + 1],
                                       scale=rstd[g % 2][:, t:t + 1]).then_inc(xg_normed, 1)
                        if t:
                            high(i - 1)
                    high(T * g + T - 1)
                if stage == "raw":
                    w, k = arg
                    r = K * w + k
                    act.wait_ge(raw_loaded[r % 2], 16 * (r // 2 + 1))
                    if w == WO:
                        act.wait_ge(product_done, K * (number[(PROD, 1)] + 1))
                    act.copy(split_into[w][0][:, k, :], raw[r % 2][:]).then_inc(raw_hi_done, 1)
                if stage == "take":
                    n = arg
                    hi, _ = result_of(n)
                    act.wait_ge(product_done, n + 1)
                    if n >= 2:
                        act.wait_ge(product_lo, n - 1)
                    if is_score(n):
                        s = n - K * number[(SCORE, 0)]
                        act.wait_ge(smax_done, s + 1)
                        act.mul(sbias[:, s:s + 1], smax[:, s:s + 1], -SCALE).then_inc(sbias_done, 1)
                        act.wait_ge(sbias_done, s + 1)
                        act.activation(full[n % 2][:], product_bank(n)[:], ACT.Exp, bias=sbias[:, s:s + 1], scale=SCALE,
                                       accum_out=ssum[:, s:s + 1]).then_inc(product_taken, 1)
                    else:
                        act.copy(hi, as_result(n, product_bank(n))).then_inc(product_hi, 1)
                        act.copy(full[n % 2][:], product_bank(n)[:]).then_inc(product_taken, 1)
                if stage == "norm":
                    n, s = arg, arg - K * number[(SCORE, 0)]
                    act.wait_ge(srec_done, s + 1)
                    act.activation(full[n % 2][:], full[n % 2][:], ACT.Copy, scale=srec[:, s:s + 1]).then_inc(snorm_done, 1)
                    act.wait_ge(snorm_done, s + 1)
                    act.copy(result_of(n)[0], full[n % 2][:]).then_inc(product_hi, 1)
                if stage == "build" and arg[1] == 3:
                    weight_high(arg[0])
                if stage == "first":
                    turn_first(arg)

            def ffn(b):
                for c in range(C):
                    n = rows(c)
                    act.wait_ge(gate_done, b.count(C, c))
                    if not (b.first and c == 0):
                        act.wait_ge(h_done, b.count(C, c - 1))
                    act.activation(h_gate[0:n, :], bank[4][0:n, :], ACT.Silu).then_inc(silu_done, 1)
                    act.wait_ge(h_done, b.count(C, c))
                    if b.first and c == 0:
                        act.wait_ge(x2_turned, K)
                    if c >= 2:
                        act.wait_ge(down_done, b.count(C, c - 2))
                    elif not b.first:
                        act.wait_ge(down_done, b.count(C, -1))
                    act.copy(h_hi[c % 2][0:n, :], h_full[0:n, :]).then_inc(h_hi_done, 1)
                    if b.first:
                        for u in late_units(c):
                            weight_high(u)
                    for step in preparation(b, c):
                        if step == "ln1":
                            act.wait_ge(x2_turned, b.count(K, K - 1))
                            normalise(b.next(), xn, 0)
                        elif step == "ln2":
                            act.wait_ge(xt_turned, b.next().count(T, T - 1))
                            normalise(b.next(), xn, 1)
                        elif step[0] == "turn":
                            x_high(b.next(), step[1])
                if not b.last:
                    x2_high(b.next())

            ffn(Block(0, 0))
            every_block(act, ffn)

        @blk.tensor
        def _(pe):
            def products(out_, terms):
                last = None
                for i, ((lh, ll), (rh, rl)) in enumerate(terms):
                    for j, (a, b) in enumerate(((lh, rh), (ll, rh), (lh, rl))):
                        last = pe.matmul(out_, a, b, start=(i == 0 and j == 0), stop=(i == len(terms) - 1 and j == 2))
                return last

            def turn_x(b, source, t):
                pe.wait_ge(ln1_done, b.count(T, t))
                if b.first and t == 0:
                    pe.wait_ge(idx_laid, U)
                elif t == 0:
                    pe.wait_ge(x2_lo_done, b.count(K, -1))
                else:
                    pe.wait_ge(xt_lo_done, b.count(T, t - 1))
                for k in range(K):
                    last = pe.transpose(bank[6][:, k * P:(k + 1) * P], source[:, t, k * P:(k + 1) * P], ident[:])
                last.then_inc(xt_turned, 1)

            def attend(b, t):
                pe.wait_ge(xt_lo_done, b.count(T, t))
                if t:
                    pe.wait_ge(x1_done, b.count(T, t - 1))
                if not (isinstance(b.n, int) and b.n < 2):
                    pe.wait_ge(m_loaded, 32 * b.half)
                products(bank[7][:], [((xt_hi[:, k, :], xt_lo[:, k, :]), (m_hi[:, k, :], m_lo[:, k, :]))
                                      for k in range(K)]).then_inc(attn_done, 1)

            def turn_x2(b, source, k):
                if k == 0:
                    pe.wait_ge(ln2_done, b.count(T, T - 1))
                if k >= 2:
                    pe.wait_ge(x2_lo_done, b.count(K, k - 2))
                for t in range(T):
                    last = pe.transpose(bank[6 + k % 2][:, t * P:(t + 1) * P], source[:, t, k * P:(k + 1) * P], ident[:])
                last.then_inc(x2_turned, 1)

            operands = {PROD: (mat_x, wa), SCORE: (wb, mat_y), MIX: (mat_x, wa), FOLD: (wb, mat_y)}
            before = {PROD: GRAM, SCORE: PROD, MIX: SCORE, FOLD: MIX}
            weight = {PROD: WK, SCORE: WQ, MIX: WO}
            pe.wait_ge(const_made, 4)
            for stage, arg in timeline:
                if stage == "idx":
                    u, c, kind = arg, arg // 3, arg % 3
                    n = rows(c)
                    pe.wait_ge(idx_cast, u + 1)
                    if u >= 4:
                        pe.wait_ge(idx_laid, u - 3)
                    if u == U_IDX_EARLY:
                        pe.wait_ge(product_taken, LAST_ITEM)
                    turned = bank[4 + u % 4][:].bitcast(BF16)
                    for k in range(K):
                        if kind < 2:
                            last = pe.transpose(turned[:, k * P:k * P + n], idx_bf[u % 2][0:n, k * P:(k + 1) * P], ident_bf[0:n, 0:n])
                        else:
                            last = pe.transpose(turned[0:n, k * P:(k + 1) * P], idx_bf[u % 2][:, k * P:k * P + n], ident_bf[:])
                    last.then_inc(idx_turned, 1)
                if stage == "gram":
                    g, batch = arg, arg // GB
                    if g == GB:
                        pe.wait_ge(idx_laid, U_IDX_EARLY)
                    for i in range(T * g, T * g + T):
                        pe.wait_ge(xg_lo_done, i + 1)
                        start, stop = i % (T * GB) == 0, i % (T * GB) == T * GB - 1
                        hi, lo = xg_hi[i % 4], xg_lo[i % 4]
                        for m in range(K):
                            rows_of = slice(m * P, (m + 1) * P)
                            for j, (a, b) in enumerate(((hi, hi), (lo, hi), (hi, lo))):
                                last = pe.matmul(bank[4 * batch + m][:], a[:, rows_of], b[:], start=start and j == 0,
                                                 stop=stop and j == 2)
                            if stop:
                                last.then_inc(product_done, 1)
                        if stop:
                            pe.wait_ge(product_done, K * (batch + 1))
                            pe.sem_inc(xg_used, 1)
                        else:
                            last.then_inc(xg_used, 1)
                if stage == "product":
                    n = arg
                    (name, b), m = groups[n // K], n % K
                    pe.wait_ge(product_taken, n - 2 * K + 1)
                    if name == TURN_V:
                        r = K * WV + m
                        pe.wait_ge(raw_loaded[r % 2], 16 * (r // 2 + 1))
                        for k in range(K):
                            last = pe.transpose(product_bank(n)[:, k * P:(k + 1) * P], raw[r % 2][:, k * P:(k + 1) * P], ident[:])
                        last.then_inc(product_done, 1)
                        continue
                    left, right = operands[name]
                    left = left[b] if name in (PROD, MIX) else left
                    right = right if name in (PROD, MIX) else right[b]
                    pe.wait_ge(product_lo, K * (number[(before[name], b)] + 1))
                    if name in weight:
                        pe.wait_ge(raw_lo_done, K * (weight[name] + 1))
                    else:
                        pe.wait_ge(product_lo, K * (number[(TURN_V, 0)] + 1))
                    products(product_bank(n)[:], [([a[:, k, m * P:(m + 1) * P] for a in left], [a[:, k, :] for a in right])
                                                  for k in range(K)]).then_inc(product_done, 1)
                if stage == "first":
                    if arg == "x2":
                        for k in range(K):
                            turn_x2(Block(0, 0), xn_first, k)
                    elif arg not in ("ln1", "ln2"):
                        turn_x(Block(0, 0), xn_first, arg)
                        attend(Block(0, 0), arg)

            def ffn(b):
                def down(c):
                    n = rows(c)
                    pe.wait_ge(h_lo_done, b.count(C, c))
                    if c == 0 and not b.first:
                        pe.wait_ge(y_added, b.count(T, -1))
                    if b.first:
                        pe.wait_ge(w_lo_done, 3 * c + 3)
                    for t in range(T):
                        tokens = slice(t * P, (t + 1) * P)
                        hi, lo = h_hi[c % 2][0:n, tokens], h_lo[c % 2][0:n, tokens]
                        w = w_hi[c][0:n, 2, :], w_lo[c][0:n, 2, :]
                        for j, (a, x) in enumerate(((hi, w[0]), (lo, w[0]), (hi, w[1]))):
                            last = pe.matmul(bank[t][:], a, x, start=(c == 0 and j == 0), stop=(c == C - 1 and j == 2))
                    last.then_inc(down_done, 1)

                for c in range(C):
                    n = rows(c)
                    if c == 0:
                        pe.wait_ge(x2_lo_done, b.count(K, K - 1))
                    for kind, done, read in ((0, gate_done, silu_done), (1, up_done, h_done)):
                        if b.first:
                            pe.wait_ge(w_lo_done, 3 * c + kind + 1)
                        if not (b.first and c == 0):
                            pe.wait_ge(read, b.count(C, c - 1))
                        products(bank[4 + kind][0:n, :],
                                 [([w[c][:, kind, k * P:k * P + n] for w in (w_hi, w_lo)], (x2t_hi[:, k, :], x2t_lo[:, k, :]))
                                  for k in range(K)]).then_inc(done, 1)
                    for step in preparation(b, c):
                        if step[0] == "turn":
                            turn_x(b.next(), xn, step[1])
                        elif step[0] == "attend":
                            attend(b.next(), step[1])
                    if c == C - 1 and not b.last:
                        turn_x2(b.next(), xn, 0)
                        turn_x2(b.next(), xn, 1)
                    if c:
                        down(c - 1)
                if not b.last:
                    turn_x2(b.next(), xn, 2)
                    turn_x2(b.next(), xn, 3)
                down(C - 1)

            ffn(Block(0, 0))
            every_block(pe, ffn)

        @blk.vector
        def _(dve):
            class Steps:
                base, n = 0, 0

            def step(ins):
                Steps.n += 1
                ins.then_inc(dve_steps, 1)
                return Steps.base + Steps.n

            def need(value):
                dve.wait_ge(dve_steps, value)

            def norm_stats(x, which, done):
                for t in range(T):
                    last = dve.bn_stats(bn[:, t, :], x[:, t, :])
                need(step(last))
                dve.memset(tmp[:], 0.0)
                for t in range(T):
                    last = dve.bn_aggr(mv[:, t, :], bn[:, t, :])
                need(step(last))
                need(step(dve.tensor_scalar(var[:], mv[:, :, 1], EPS, None, ALU.add)))
                y = rstd[which]
                need(step(dve.tensor_scalar(y[:].bitcast(I32), var[:].bitcast(I32), -0.5, RSQRT_SEED, ALU.mult, ALU.add)))
                for _ in range(NEWTON):
                    need(step(dve.tensor_tensor(tmp[:], y[:], y[:], ALU.mult)))
                    need(step(dve.scalar_tensor_tensor(out=tmp[:], in0=tmp[:], scalar=-0.5, in1=var[:], op0=ALU.mult, op1=ALU.mult)))
                    need(step(dve.scalar_tensor_tensor(out=y[:], in0=tmp[:], scalar=1.5, in1=y[:], op0=ALU.add, op1=ALU.mult)))
                dve.scalar_tensor_tensor(out=shift[which][:], in0=mv[:, :, 0], scalar=-1.0, in1=y[:], op0=ALU.mult,
                                         op1=ALU.mult).then_inc(done, 1)

            STEPS_PER_NORM = 4 + 3 * NEWTON

            def leaf(tile, j, used=None):
                if used is not None:
                    need(used)
                return step(dve.tensor_scalar(tile[:].bitcast(I32), high_mask[:], lut_x[:, j:j + 1], lut[:, j:j + 1].bitcast(I32),
                                              ALU.bitwise_and, ALU.bitwise_xor))

            def merge(bit, keep, other, ready):
                need(ready)
                return step(dve.copy_predicated(keep[:], bit_mask[bit][:], other[:]))

            def build_quarter(u, q, made):
                r, (x, y, z, w) = picked[u % 2], part
                c, kind = u // 3, u % 3
                if q == 0:
                    dve.wait_ge(idx_laid, u + 1)
                    if u >= 1:
                        dve.wait_ge(picked_done, u)
                    if u >= 2:
                        dve.wait_ge(w_lo_done, u - 1)
                    idx = idx_t[c][:, kind, :]
                    mask = step(dve.tensor_scalar(high_mask[:], idx, float(HALF), -1.0, ALU.is_ge, ALU.mult))
                    for bit in range(3):
                        step(dve.tensor_scalar(bit_mask[bit][:], idx, 1 << bit, None, ALU.bitwise_and))
                    need(mask)
                    leaf(r, 0)
                    made["x"] = leaf(x, 1)
                if q == 1:
                    leaf(y, 2)
                    z3 = leaf(z, 3)
                    made["rx"] = merge(0, r, x, made["x"])
                    made["yz"] = merge(0, y, z, z3)
                if q == 2:
                    leaf(x, 4, made["rx"])
                    made["ry"] = merge(1, r, y, made["yz"])
                    w5 = leaf(w, 5)
                    leaf(z, 6)
                    made["xw"] = merge(0, x, w, w5)
                if q == 3:
                    y7 = leaf(y, 7, made["ry"])
                    zy = merge(0, z, y, y7)
                    xz = merge(1, x, z, zy)
                    need(xz)
                    dve.copy_predicated(r[:], bit_mask[2][:], x[:]).then_inc(picked_done, 1)

            def x_low(b, t):
                dve.wait_ge(xt_hi_done, b.count(T, t))
                dve.tensor_tensor(xt_lo[:].rearrange("p k s -> p (k s)"), bank[6][:],
                                  xt_hi[:].rearrange("p k s -> p (k s)").bitcast(F32), ALU.subtract).then_inc(xt_lo_done, 1)

            def add_attention(b, t):
                dve.wait_ge(attn_done, b.count(T, t))
                dve.wait_ge(ln1_done, b.count(T, t))
                dve.tensor_tensor(x1[b.parity][:, t, :], bank[7][:], x1[b.parity][:, t, :], ALU.add).then_inc(x1_done, 1)

            def x2_low(b):
                for k in range(K):
                    dve.wait_ge(x2_hi_done, b.count(K, k))
                    dve.tensor_tensor(x2t_lo[:, k, :], bank[6 + k % 2][:], x2t_hi[:, k, :].bitcast(F32),
                                      ALU.subtract).then_inc(x2_lo_done, 1)

            def stats1(b):
                dve.wait_ge(x_loaded[b.parity], 16 * (b.half + 1))
                if not b.first:
                    dve.wait_ge(ln1_done, b.count(T, -1))
                norm_stats(x1[b.parity], 0, ln1_stats)

            def stats2(b):
                dve.wait_ge(x1_done, b.count(T, T - 1))
                if not b.first:
                    dve.wait_ge(ln2_done, b.count(T, -1))
                norm_stats(x1[b.parity], 1, ln2_stats)

            first = Block(0, 0)
            made = {}
            dve.wait_ge(lut_loaded, 16)
            need(step(dve.tensor_tensor(lut_x[:], lut[:, 0:HALF].bitcast(I32), lut[:, HALF:LUT].bitcast(I32), ALU.bitwise_xor)))
            for stage, arg in timeline:
                if stage == "gram":
                    g = arg
                    dve.wait_ge(xg_loaded[g % 2], 16 * (g // 2 + 1))
                    if g >= 2:
                        dve.wait_ge(xg_normed, T * (g - 1))
                    norm_stats(xg[g % 2], g % 2, xg_stats)
                if stage == "take" and is_score(arg):
                    s = arg - K * number[(SCORE, 0)]
                    dve.wait_ge(product_done, arg + 1)
                    dve.reduce_max(smax[:, s:s + 1], product_bank(arg)[:], AX_X).then_inc(smax_done, 1)
                if stage == "norm":
                    s = arg - K * number[(SCORE, 0)]
                    dve.wait_ge(product_taken, arg + 1)
                    dve.reciprocal(srec[:, s:s + 1], ssum[:, s:s + 1]).then_inc(srec_done, 1)
                if stage == "build":
                    build_quarter(*arg, made)
                if stage == "first":
                    if arg == "ln1":
                        dve.wait_ge(xg_normed, T * NG)
                        stats1(first)
                    elif arg == "ln2":
                        stats2(first)
                    elif arg == "x2":
                        x2_low(first)
                    else:
                        x_low(first, arg)
                        add_attention(first, arg)

            def ffn(b):
                for c in range(C):
                    n = rows(c)
                    dve.wait_ge(up_done, b.count(C, c))
                    dve.wait_ge(silu_done, b.count(C, c))
                    if not (b.first and c == 0):
                        dve.wait_ge(h_lo_done, b.count(C, c - 1))
                    dve.tensor_tensor(h_full[0:n, :], bank[5][0:n, :], h_gate[0:n, :], ALU.mult).then_inc(h_done, 1)
                    if b.first:
                        for u in late_units(c):
                            for q in range(4):
                                build_quarter(u, q, made)
                    for s in preparation(b, c):
                        if s == "stats1":
                            stats1(b.next())
                        elif s == "stats2":
                            stats2(b.next())
                        elif s[0] == "turn":
                            x_low(b.next(), s[1])
                        elif s[0] == "attend":
                            add_attention(b.next(), s[1])
                if not b.last:
                    x2_low(b.next())
                dve.wait_ge(down_done, b.count(C, C - 1))
                for t in range(T):
                    dve.tensor_tensor(x1[b.parity][:, t, :], bank[t][:], x1[b.parity][:, t, :], ALU.add).then_inc(y_added, 1)

            ffn(first)
            begun, pairs = Steps.n, (NG - 2) // 2
            with dve.Fori(0, pairs) as j:
                Steps.base, Steps.n = 4 * STEPS_PER_NORM * j, begun
                ffn(Block(j, 1))
                ffn(Block(j, 2))
            assert Steps.n == begun + 4 * STEPS_PER_NORM
            Steps.base, Steps.n = 0, begun + 4 * STEPS_PER_NORM * pairs
            ffn(Block(0, NG - 1))


_INS = ["L0_attn_x", "L0_attn_Wq", "L0_attn_Wk", "L0_attn_Wv", "L0_attn_Wo", "L0_ffn_lut", "L0_ffn_gate_idx",
        "L0_ffn_up_idx", "L0_ffn_down_idx"]
_ARGS = ["x_in", "wq_in", "wk_in", "wv_in", "wo_in", "lut_in", "gate_in", "up_in", "down_in"]


def kernel(**inputs):
    import numpy as _np
    import concourse.bacc as _bacc
    from concourse import mybir as _mybir
    from concourse.bass_utils import run_bass_kernel_spmd as _run

    nc = _bacc.Bacc("TRN2", target_bir_lowering=False, num_devices=1)
    arrays, args = {}, {}
    for name, arg in zip(_INS, _ARGS):
        a = _np.ascontiguousarray(inputs[name])
        arrays[f"in_{name}"] = a
        args[arg] = nc.dram_tensor(f"in_{name}", a.shape, _mybir.dt.from_np(a.dtype), kind="ExternalInput").ap()
    shape = arrays["in_L0_attn_x"].shape
    out = nc.dram_tensor("out_dram", shape, _mybir.dt.float32, kind="ExternalOutput").ap()
    preln_attention_ghost_ffn(nc, out=out, **args)
    r = _run(nc, [arrays], core_ids=[0])
    return r.results[0]["out_dram"]
```

```python
from contextlib import ExitStack

import concourse.bass as bass
from concourse import mybir
from concourse.alu_op_type import AluOpType as ALU

ACT = mybir.ActivationFunctionType
AX_X = mybir.AxisListType.X
F32 = mybir.dt.float32
F32R = mybir.dt.float32r
BF16 = mybir.dt.bfloat16
I16 = mybir.dt.int16
I32 = mybir.dt.int32
U8 = mybir.dt.uint8

P = 128
EPS = 1e-5
RSQRT_SEED = float(0x5F3759DF)
NEWTON = 3
KIB = 1024


def preln_attention_ghost_ffn(nc, x_in, wq_in, wk_in, wv_in, wo_in, lut_in, gate_in, up_in, down_in, out):
    B, S, D = x_in.shape
    I = gate_in.shape[0]
    LUT = lut_in.shape[0]
    K = D // P
    T = 4
    BT = T * P
    NG = B * S // BT
    GB = S // BT
    C = -(-I // P)
    HALF = LUT // 2
    HIGH_BIT = 3
    SCALE = 1.0 / float((D // 32) ** 0.5)

    def rows(c):
        return min(P, I - c * P)

    U = 3 * C
    LOOKS_GRAM, LOOKS_CHAIN = 3, 4
    LATE_SLOTS = 8
    LOOKS_FIRST = 8, 8, 8, 8
    assert (D, K, C, NG, GB, LUT) == (512, 4, 11, 8, 4, 16)

    xb_dram = x_in.rearrange("b s d -> (b s) d").rearrange("(n p t) d -> n p t d", p=P, t=T)
    ob_dram = out.rearrange("b s d -> (b s) d").rearrange("(n p t) d -> n p t d", p=P, t=T)

    ctx = ExitStack()
    with ctx:
        base = 16512

        def at(name, kib, shape, dt):
            return nc.alloc_sbuf_tensor_at(name, shape, dt, offset=base + int(kib * KIB))

        def sem(name):
            return ctx.enter_context(nc.semaphore(name))

        w_at = [12 * c + (8 if c >= 8 else 0) for c in range(C)]
        w_hi = [at(f"w_hi{c}", w_at[c], [P, 3, D], F32R) for c in range(C)]
        w_lo = [at(f"w_lo{c}", w_at[c] + 6, [P, 3, D], F32R) for c in range(C)]
        x2t_hi = at("x2t_hi", 140, [P, K, BT], F32R)
        x2t_lo = at("x2t_lo", 148, [P, K, BT], F32R)
        m_hi = at("m_hi", 156, [P, K, D], F32R)
        m_lo = at("m_lo", 164, [P, K, D], F32R)
        x1 = [at("x1a", 96, [P, T, D], F32), at("x1b", 188, [P, T, D], F32)]
        h_hi = [at(f"h_hi{i}", 172 + 4 * i, [P, BT], F32R) for i in range(2)]
        h_lo = [at(f"h_lo{i}", 174 + 4 * i, [P, BT], F32R) for i in range(2)]
        h_gate = at("h_gate", 180, [P, BT], F32)
        h_full = at("h_full", 182, [P, BT], F32)
        xt_hi = [at(f"xt_hi{i}", 184 - 4 * i, [P, K, P], F32R) for i in range(2)]
        xt_lo = [at(f"xt_lo{i}", 186 - 4 * i, [P, K, P], F32R) for i in range(2)]
        xn = at("xn", 196, [P, T, D], F32)
        xn_first = at("xn_first", 172, [P, T, D], F32)
        mat_x = [(at(f"mat_x_hi{b}", 60 + 32 * b, [P, K, D], F32R), at(f"mat_x_lo{b}", 68 + 32 * b, [P, K, D], F32R)) for b in range(B)]
        mat_y = [(at(f"mat_y_hi{b}", 76 + 32 * b, [P, K, D], F32R), at(f"mat_y_lo{b}", 84 + 32 * b, [P, K, D], F32R)) for b in range(B)]
        wa = (at("wa_hi", 132, [P, K, D], F32R), at("wa_lo", 140, [P, K, D], F32R))
        wb = (at("wb_hi", 148, [P, K, D], F32R), at("wb_lo", 124, [P, K, D], F32R))
        raw = [at(f"raw{i}", 184 + 2 * i, [P, D], F32) for i in range(2)]
        full = [at(f"full{i}", 180 + 2 * i, [P, D], F32) for i in range(2)]
        xg = [at(f"xg{i}", kib, [P, T, D], F32) for i, kib in enumerate((76, 84, 156))]
        xg_hi = [at(f"xg_hi{i}", 108 + 4 * i, [P, D], F32R) for i in range(4)]
        xg_lo = [at(f"xg_lo{i}", 110 + 4 * i, [P, D], F32R) for i in range(4)]
        xg_n = [at(f"xg_n{i}", 164 + 2 * i, [P, D], F32) for i in range(4)]
        idx_raw = [at(f"idx_raw{i}", 92 + 2 * i, [P, D], I32) for i in range(8)]
        idx_bf = [at(f"idx_bf{i}", 172 + 1 * i, [P, D], BF16) for i in range(4)]
        idx_out = [at(f"idx_out{i}", 176 + i / 2, [P, D], U8) for i in range(4)]
        picked = [at("picked0", 188, [P, D], F32), at("picked1", 190, [P, D], F32)]
        part = [at(f"part{i}", kib, [P, D], F32) for i, kib in enumerate((192, 194, 196, 198, 205.75))]
        high_bit = [at(f"high_bit{i}", 203 + i / 2, [P, D], U8) for i in range(2)]
        bit_mask = [at(f"bit_mask{i}", 200 + i / 2, [P, D], U8) for i in range(3)]
        idx_in = [at(f"idx_in{i}", 201.5 + i / 2, [P, D], U8) for i in range(3)]
        ident = at("ident", 204, [P, P], F32)
        ident_bf = at("ident_bf", 204.5, [P, P], BF16)
        lut = at("lut", 204.75, [P, LUT], F32)
        lut_step = at("lut_step", 204.8125, [P, HALF], F32)
        bn = at("bn", 204.875, [P, T, 6], F32)
        mv = at("mv", 205, [P, T, 2], F32)
        var = at("var", 205.0625, [P, T], F32)
        tmp = at("tmp", 205.125, [P, T], F32)
        rstd = [at(f"rstd{i}", 205.1875 + i / 16, [P, T], F32) for i in range(2)]
        shift = [at(f"shift{i}", 205.3125 + i / 16, [P, T], F32) for i in range(2)]
        smax = at("smax", 205.4375, [P, 2 * K], F32)
        sbias = at("sbias", 205.5, [P, 2 * K], F32)
        ssum = at("ssum", 205.5625, [P, 2 * K], F32)
        srec = at("srec", 205.625, [P, 2 * K], F32)

        bank = [ctx.enter_context(nc.psum_tensor(f"bank{i}", [P, D], F32)) for i in range(8)]
        idx_dram = nc.dram_tensor("idx_scratch", (U, P, D), U8).ap()
        m_dram = nc.dram_tensor("m_scratch", (B, 2, P, K * D), F32).ap()

        const_made = sem("const_made")
        lut_loaded = sem("lut_loaded")
        dve_steps = sem("dve_steps")
        idx_loaded = [sem(f"idx_loaded{i}") for i in range(8)]
        idx_cast = sem("idx_cast")
        idx_turned = sem("idx_turned")
        idx_laid = sem("idx_laid")
        idx_stored = [sem(f"idx_stored{i}") for i in range(4)]
        idx_back = [sem(f"idx_back{i}") for i in range(3)]
        step_made = sem("step_made")
        high_made = sem("high_made")
        leaf_made = sem("leaf_made")
        merged = sem("merged")
        idx_cleared = sem("idx_cleared")
        mirrored = sem("mirrored")
        mirror_taken = sem("mirror_taken")
        picked_done = sem("picked_done")
        w_hi_done = sem("w_hi_done")
        w_lo_done = sem("w_lo_done")
        xg_loaded = [sem(f"xg_loaded{i}") for i in range(3)]
        xg_stats = sem("xg_stats")
        xg_normed = sem("xg_normed")
        xg_hi_done = sem("xg_hi_done")
        xg_lo_done = sem("xg_lo_done")
        xg_used = sem("xg_used")
        raw_loaded = [sem(f"raw_loaded{i}") for i in range(2)]
        raw_hi_done = sem("raw_hi_done")
        raw_lo_done = sem("raw_lo_done")
        product_done = sem("product_done")
        product_taken = sem("product_taken")
        product_hi = sem("product_hi")
        product_lo = sem("product_lo")
        smax_done = sem("smax_done")
        sbias_done = sem("sbias_done")
        sexp_done = sem("sexp_done")
        srec_done = sem("srec_done")
        snorm_done = sem("snorm_done")
        m_stored = sem("m_stored")
        m_loaded = sem("m_loaded")
        x_loaded = [sem(f"x_loaded{i}") for i in range(2)]
        out_stored = [sem(f"out_stored{i}") for i in range(2)]
        ln1_stats = sem("ln1_stats")
        ln1_done = sem("ln1_done")
        xt_turned = sem("xt_turned")
        xt_hi_done = sem("xt_hi_done")
        xt_lo_done = sem("xt_lo_done")
        attn_done = sem("attn_done")
        x1_done = sem("x1_done")
        ln2_stats = sem("ln2_stats")
        ln2_done = sem("ln2_done")
        x2_turned = sem("x2_turned")
        x2_hi_done = sem("x2_hi_done")
        x2_lo_done = sem("x2_lo_done")
        gate_done = sem("gate_done")
        up_done = sem("up_done")
        silu_done = sem("silu_done")
        h_done = sem("h_done")
        h_hi_done = sem("h_hi_done")
        h_lo_done = sem("h_lo_done")
        down_done = sem("down_done")
        y_added = sem("y_added")

        GRAM, PROD, SCORE, TURN_V, MIX, FOLD = "gram", "prod", "score", "turn_v", "mix", "fold"
        groups = [(GRAM, 0), (GRAM, 1), (PROD, 0), (PROD, 1), (SCORE, 0), (SCORE, 1),
                  (TURN_V, 0), (MIX, 0), (MIX, 1), (FOLD, 0), (FOLD, 1)]
        number = {g: q for q, g in enumerate(groups)}
        LAST_ITEM = K * len(groups)
        WK, WQ, WO, WV = range(4)
        raws = [wk_in, wq_in, wo_in, wv_in]
        split_into = {WK: wa, WQ: wb, WO: wa}

        def product_bank(n):
            return bank[4 * (n // K % 2) + n % K]

        def result_of(n):
            (name, b), m = groups[n // K], n % K
            if name == TURN_V:
                return [a[:, :, m * P:(m + 1) * P] for a in wb]
            pair = {GRAM: mat_x[b], SCORE: mat_x[b], PROD: mat_y[b], MIX: mat_y[b],
                    FOLD: (m_hi, m_lo) if b == 0 else wa}[name]
            first = gram_first(m) if name == GRAM else 0
            return [a[:, m, first:] for a in pair]

        def as_result(n, tile):
            name, m = groups[n // K][0], n % K
            if name == TURN_V:
                return tile[:].rearrange("p (k d) -> p k d", k=K)
            return tile[:, gram_first(m):] if name == GRAM else tile[:]

        def gram_first(m):
            return P * min(m, K - 2)

        def is_score(n):
            return groups[n // K][0] == SCORE

        OPS = 12
        LEAVES = [2, 3, 1, 5, 4, 7, 6]
        LEAVES_NEXT = {5: [2, 3], 6: [1, 5], 9: [4]}
        LEAVES_SAME = {0: [7], 1: [6]}
        tile_of_leaf = {1: 0, 2: 1, 3: 2, 4: 3, 5: 4, 6: 0, 7: 2}
        M_YZ, M_RX, M_WV, M_RY, M_XZ, M_WX = range(6)
        MERGES = 6

        def merge_count(u, which):
            return MERGES * u + which + 1

        def leaf_count(u, j):
            return len(LEAVES) * u + LEAVES.index(j) + 1

        timeline = []
        looked = [0]

        def look(n, limit):
            for _ in range(min(n, OPS * limit - looked[0])):
                timeline.append(("look", looked[0]))
                looked[0] += 1
                if looked[0] % OPS == 0:
                    timeline.append(("built", looked[0] // OPS - 1))

        def room(n):
            return 15 if n < K * (number[(MIX, 0)] + 1) else 18 if n < K * (number[(FOLD, 0)] + 1) else 24

        idx_per_tile = [1 + (i % 4 == 3) if i < T * GB else (i >= T * GB + 4) + (i == T * NG - 1) for i in range(T * NG)]
        assert sum(idx_per_tile) == U
        MIRROR_AT = T * NG - 4
        U_HIGH_BANKS = sum(idx_per_tile[0:T * GB])
        U_BEFORE_MIRROR = sum(idx_per_tile[0:MIRROR_AT])
        AHEAD = 2
        timeline += [("cast", u) for u in range(3)] + [("stats", 0)] + [("gram_in", i) for i in range(AHEAD)]
        u = 0
        for i in range(T * NG):
            if i % T == 0 and i // T + 1 < NG:
                timeline.append(("stats", i // T + 1))
            if i + AHEAD < T * NG:
                timeline.append(("gram_in", i + AHEAD))
            for _ in range(idx_per_tile[i]):
                timeline += ([("cast", u + 3)] if u + 3 < U else []) + [("idx", u)]
                u += 1
            timeline.append(("gram", i))
            if T * GB <= i < T * GB + K:
                timeline.append(("take", i - T * GB))
            if 12 <= i < 28 and i % 2 == 0:
                timeline.append(("raw", divmod((i - 12) // 2, K)))
            if i == MIRROR_AT - 1:
                timeline.append(("mirror", 0))
            look(LOOKS_GRAM if i >= 8 else 0, 15)
        for n in range(K, LAST_ITEM):
            if n == K * number[(PROD, 1)]:
                timeline.append(("mirror", 1))
            if n >= 2 * K:
                timeline.append(("product", n))
            if n == K * number[(FOLD, 1)]:
                timeline += [("first", "stats1"), ("first", "ln1")]
            timeline.append(("take", n))
            if is_score(n):
                if is_score(n - 1):
                    timeline.append(("norm", n - 1))
                if not is_score(n + 1):
                    timeline.append(("norm", n))
                if n < K * (number[(SCORE, 0)] + 1):
                    timeline.append(("raw", (WO, n % K)))
            if groups[n // K] == (FOLD, 1):
                t = n % K
                timeline += ([("first", ("attend", t - 1))] if t else []) + [("first", ("turn", t))]
                look(LOOKS_FIRST[0], room(n))
            else:
                look(LOOKS_CHAIN, room(n))
        look(LOOKS_FIRST[1], room(n))
        timeline += [("first", ("attend", T - 1)), ("first", "stats2")]
        look(LOOKS_FIRST[2], U)
        timeline.append(("first", "ln2"))
        look(LOOKS_FIRST[3], U)
        timeline.append(("first", "x2"))
        early = looked[0]

        def late_looks(c):
            if c >= LATE_SLOTS:
                return range(0)
            n = OPS * U - early
            return range(early + n * c // LATE_SLOTS, early + n * (c + 1) // LATE_SLOTS)

        for c in range(1, C):
            assert late_looks(c - 1).stop >= 3 * OPS * (c + 1) or c > LATE_SLOTS or early >= 3 * OPS * (c + 1)

        def built_by(k):
            return [k // OPS] if k % OPS == OPS - 1 else []

        def idx_bank(u):
            return bank[(4 if u < U_HIGH_BANKS else 0) + u % 4][:].bitcast(BF16)

        class Block:

            def __init__(self, j, off):
                self.j, self.off = j, off
                fixed = isinstance(j, int)
                self.n = 2 * j + off
                self.first = fixed and self.n == 0
                self.last = fixed and self.n == NG - 1
                self.parity = off % 2
                self.half = j + off // 2
                self.between = fixed and self.n == 1

            def next(self):
                return None if self.last else Block(self.j, self.off + 1)

            def count(self, per, i):
                return per * self.n + (i + 1)

            def xt(self, t):
                return t % 2 if self.between else 0

            def turn_bank(self, t):
                return bank[(6, 4)[self.xt(t)]]

        LN1_STATS, LN1, TURN, LN2 = 1, 2, 3, 8
        FIRST_STATS = 9

        def preparation(b, c):
            if b.last:
                return []
            if b.first:
                return {FIRST_STATS: ["stats1"], C - 1: ["ln1", ("turn", 0), ("turn", 1), "down", ("attend", 0), ("turn", 2),
                        ("attend", 1), ("turn", 3), ("attend", 2), "last down", ("attend", 3), "stats2", "ln2"]}.get(c, [])
            steps = {LN1_STATS: ["stats1"], LN1: ["ln1"], LN2: ["ln2"], TURN + T: [("attend", T - 1), "stats2"]}
            for t in range(T):
                if TURN + t <= c and c == TURN + t:
                    return ([("attend", t - 1)] if t else []) + [("turn", t)]
            return steps.get(c, [])

        def every_block(eng, run):
            with eng.Fori(0, (NG - 2) // 2) as j:
                run(Block(j, 1))
                run(Block(j, 2))
            run(Block(0, NG - 1))

        blk = ctx.enter_context(nc.Block())

        @blk.sync
        def _(sp):
            def load_idx(u):
                c, kind = u // 3, u % 3
                if u >= 8:
                    sp.wait_ge(idx_cast, u - 7)
                n = rows(c)
                if kind < 2:
                    src = (gate_in, up_in)[kind][c * P:c * P + n, :]
                    sp.dma_start(idx_raw[u % 8][0:n, :], src).then_inc(idx_loaded[u % 8], 16)
                else:
                    src = down_in[:, c * P:c * P + n].rearrange("(k p) i -> p k i", p=P)
                    dst = idx_raw[u % 8][:, :].rearrange("p (k i) -> p k i", k=K)[:, :, 0:n]
                    sp.dma_start(dst, src).then_inc(idx_loaded[u % 8], 16)

            def store_idx(u):
                sp.wait_ge(idx_laid, u + 1)
                sp.dma_start(idx_dram[u], idx_out[u % 4][:]).then_inc(idx_stored[u % 4], 16)

            def load_raw(w, k):
                r = K * w + k
                if r >= K * WV + 2:
                    sp.wait_ge(product_done, K * number[(TURN_V, 0)] + r - K * WV - 1)
                elif r >= 2:
                    sp.wait_ge(raw_lo_done, r - 1)
                sp.dma_start(raw[r % 2][:], raws[w][k * P:(k + 1) * P, :]).then_inc(raw_loaded[r % 2], 16)

            def load_gram(g):
                if g >= 3:
                    sp.wait_ge(xg_normed, T * (g - 2))
                sp.dma_start(xg[g % 3][:], xb_dram[g]).then_inc(xg_loaded[g % 3], 16)

            load_gram(0)
            for u in range(4):
                load_idx(u)
            load_gram(1)
            for u in range(4, 8):
                load_idx(u)
            load_gram(2)
            for stage, arg in timeline:
                if stage == "idx":
                    if arg + 8 < U:
                        load_idx(arg + 8)
                    if arg:
                        store_idx(arg - 1)
                if stage == "gram" and arg % T == 2 and arg // T + 3 < NG:
                    load_gram(arg // T + 3)
                if stage == "raw":
                    if arg == (WO, 0):
                        store_idx(U - 1)
                    load_raw(*arg)
            load_raw(WV, 0)
            load_raw(WV, 1)
            load_raw(WV, 2)
            load_raw(WV, 3)

            def flat(tile):
                return tile[:].rearrange("p k d -> p (k d)").bitcast(F32)

            def load_x(b):
                sp.dma_start(x1[b.parity][:], xb_dram[b.n]).then_inc(x_loaded[b.parity], 16)

            def store(b):
                sp.wait_ge(y_added, b.count(T, T - 1))
                sp.dma_start(ob_dram[b.n], x1[b.parity][:]).then_inc(out_stored[b.parity], 16)

            def reload_x(b):
                sp.wait_ge(out_stored[b.parity], 16 * b.half)
                load_x(b)

            def load_m(b):
                sp.wait_ge(attn_done, T * b.n)
                for i, half in enumerate((m_hi, m_lo)):
                    sp.dma_start(flat(half), m_dram[b.half // (GB // 2), i]).then_inc(m_loaded, 16)

            sp.wait_ge(product_done, K * (number[(MIX, 1)] + 1))
            load_x(Block(0, 0))
            for b, pair in enumerate(((m_hi, m_lo), wa)):
                sp.wait_ge(product_lo, K * (number[(FOLD, b)] + 1))
                for i in range(2):
                    sp.dma_start(m_dram[b, i], flat(pair[i])).then_inc(m_stored, 16)
            sp.wait_ge(w_lo_done, U)
            load_x(Block(0, 1))
            sp.wait_ge(m_stored, 16 * 2 * B)
            store(Block(0, 0))
            reload_x(Block(0, 2))
            with sp.Fori(0, (NG - 4) // 2) as j:
                load_m(Block(j, 2))
                store(Block(j, 1))
                reload_x(Block(j, 3))
                store(Block(j, 2))
                reload_x(Block(j, 4))
            load_m(Block(0, NG - 2))
            store(Block(0, NG - 3))
            reload_x(Block(0, NG - 1))
            store(Block(0, NG - 2))
            store(Block(0, NG - 1))
            for i in range(2):
                sp.wait_ge(out_stored[i], 16 * (NG // 2))

        @blk.gpsimd
        def _(pool):
            pool.dma_start(lut[:], lut_in.rearrange("(a n) -> a n", a=1).to_broadcast([P, LUT])).then_inc(lut_loaded, 16)
            pool.memset(ident[:], 0.0).then_inc(const_made, 1)
            pool.memset(ident_bf[:], 0.0).then_inc(const_made, 1)
            for tile in idx_out:
                pool.memset(tile[:], 0).then_inc(idx_cleared, 1)
            pool.wait_ge(const_made, 2)
            for one in (ident, ident_bf):
                pool.affine_select(out=one[:], in_=one[:], compare_op=ALU.not_equal, fill=1.0, base=0,
                                   pattern=[[-1, P]], channel_multiplier=1).then_inc(const_made, 1)

            def low(out_, whole, high):
                return pool.tensor_tensor(out_, whole, high.bitcast(F32), ALU.subtract)

            def weight_low(u):
                c, kind = u // 3, u % 3
                pool.wait_ge(w_hi_done, u + 1)
                low(w_lo[c][:, kind, :], picked[u % 2][:], w_hi[c][:, kind, :]).then_inc(w_lo_done, 1)

            for stage, arg in timeline:
                if stage == "gram_in":
                    i = arg
                    pool.wait_ge(xg_hi_done, i + 1)
                    low(xg_lo[i % 4][:], xg_n[i % 4][:], xg_hi[i % 4][:]).then_inc(xg_lo_done, 1)
                if stage == "raw":
                    w, k = arg
                    r = K * w + k
                    pool.wait_ge(raw_hi_done, r + 1)
                    hi, lo = split_into[w]
                    low(lo[:, k, :], raw[r % 2][:], hi[:, k, :]).then_inc(raw_lo_done, 1)
                if (stage == "take" and not is_score(arg)) or stage == "norm":
                    hi, lo = result_of(arg)
                    pool.wait_ge(product_hi, arg + 1)
                    pool.wait_ge(product_taken, arg + 1)
                    low(lo, as_result(arg, full[arg % 2]), hi).then_inc(product_lo, 1)
                if stage == "built":
                    weight_low(arg)

            def ffn(b):
                for c in range(C):
                    n = rows(c)
                    pool.wait_ge(h_hi_done, b.count(C, c))
                    low(h_lo[c % 2][0:n, :], h_full[0:n, :], h_hi[c % 2][0:n, :]).then_inc(h_lo_done, 1)
                    if b.first:
                        for k in late_looks(c):
                            for u in built_by(k):
                                weight_low(u)

            ffn(Block(0, 0))
            every_block(pool, ffn)

        @blk.scalar
        def _(act):
            def fetch_idx(u):
                act.wait_ge(idx_stored[u % 4], 16 * (u // 4 + 1))
                act.dma_start(idx_in[u % 3][:], idx_dram[u]).then_inc(idx_back[u % 3], 16)

            def make_leaf(u, j):
                if u >= U:
                    return
                tile = part[tile_of_leaf[j]]
                act.wait_ge(high_made, u + 1)
                if u and j in (1, 2, 3, 5):
                    act.wait_ge(merged, merge_count(u - 1, {1: M_WX, 2: M_RY, 3: M_XZ, 5: M_WV}[j]))
                if u and j == 4:
                    act.wait_ge(picked_done, u)
                if j in (6, 7):
                    act.wait_ge(merged, merge_count(u, {6: M_RX, 7: M_YZ}[j]))
                act.activation(tile[:], high_bit[u % 2][:], ACT.Identity, bias=lut[:, j:j + 1],
                               scale=lut_step[:, j:j + 1]).then_inc(leaf_made, 1)

            def make_leaves(k):
                u, p = divmod(k, OPS)
                if k == 0:
                    act.wait_ge(step_made, 1)
                    for j in LEAVES[0:5]:
                        make_leaf(0, j)
                for j in LEAVES_SAME.get(p, []):
                    make_leaf(u, j)
                for j in LEAVES_NEXT.get(p, []):
                    make_leaf(u + 1, j)

            def weight_high(u):
                c, kind = u // 3, u % 3
                act.wait_ge(picked_done, u + 1)
                if u + 3 < U:
                    fetch_idx(u + 3)
                if u == 15:
                    act.wait_ge(product_done, K * (number[(MIX, 0)] + 1))
                if u == 18:
                    act.wait_ge(product_done, K * (number[(FOLD, 0)] + 1))
                if u == 24:
                    act.wait_ge(product_done, LAST_ITEM)
                if u == 30:
                    act.wait_ge(m_stored, 16 * 2 * B)
                act.copy(w_hi[c][:, kind, :], picked[u % 2][:]).then_inc(w_hi_done, 1)

            def turn_first(step):
                b = Block(0, 0)
                if step == "ln1":
                    for i in range(4):
                        act.wait_ge(idx_stored[i], 16 * ((U - 1 - i) // 4 + 1))
                    normalise(b, xn_first, 0)
                elif step == "ln2":
                    normalise(b, xn_first, 1)
                elif step == "x2":
                    act.wait_ge(product_lo, LAST_ITEM)
                    x2_high(b)
                elif step[0] == "turn":
                    x_high(b, step[1])

            def normalise(b, into, second):
                stats, done = ((ln1_stats, ln1_done), (ln2_stats, ln2_done))[second]
                act.wait_ge(stats, b.count(1, 0))
                for t in range(T):
                    act.activation(into[:, t, :], x1[b.parity][:, t, :], ACT.Identity, bias=shift[second][:, t:t + 1],
                                   scale=rstd[second][:, t:t + 1]).then_inc(done, 1)

            def x_high(b, t):
                act.wait_ge(xt_turned, b.count(T, t))
                if b.between and t == 1:
                    act.wait_ge(h_lo_done, C)
                elif b.first and t == 0:
                    act.wait_ge(product_done, K * (number[(TURN_V, 0)] + 1))
                else:
                    act.wait_ge(attn_done, b.count(T, t - (2 if b.between and t else 1)))
                act.copy(xt_hi[b.xt(t)][:].rearrange("p k s -> p (k s)"), b.turn_bank(t)[:]).then_inc(xt_hi_done, 1)

            def x2_high(b):
                if b.first:
                    act.wait_ge(m_stored, 16 * 2 * B)
                for k in range(K):
                    act.wait_ge(x2_turned, b.count(K, k))
                    act.copy(x2t_hi[:, k, :], bank[6 + k % 2][:]).then_inc(x2_hi_done, 1)

            for stage, arg in timeline:
                if stage == "idx":
                    u, c, kind = arg, arg // 3, arg % 3
                    n = rows(c)
                    act.wait_ge(idx_turned, u + 1)
                    if u == 0:
                        act.wait_ge(idx_cleared, 4)
                    if u >= 4:
                        act.wait_ge(idx_stored[u % 4], 16 * (u // 4))
                    src = idx_bank(u)[:, 0:D].rearrange("p (k i) -> p k i", k=K)
                    dst = idx_out[u % 4][:].rearrange("p (k i) -> p k i", k=K)
                    if kind < 2:
                        src, dst = src[:, :, 0:n], dst[:, :, 0:n]
                    else:
                        src, dst = src[0:n], dst[0:n]
                    act.copy(dst, src).then_inc(idx_laid, 1)
                    if 4 <= u < 7:
                        fetch_idx(u - 4)
                if stage == "gram_in":
                    i = arg
                    g, t = i // T, i % T
                    act.wait_ge(xg_stats, g + 1)
                    if i >= 4:
                        act.wait_ge(xg_lo_done, i - 3)
                    act.activation(xg_n[i % 4][:], xg[g % 3][:, t, :], ACT.Identity, bias=shift[g % 2][:, t:t + 1],
                                   scale=rstd[g % 2][:, t:t + 1]).then_inc(xg_normed, 1)
                    act.wait_ge(xg_normed, i + 1)
                    if i >= 4:
                        act.wait_ge(xg_used, i - 3)
                    act.copy(xg_hi[i % 4][:], xg_n[i % 4][:]).then_inc(xg_hi_done, 1)
                if stage == "raw":
                    w, k = arg
                    r = K * w + k
                    act.wait_ge(raw_loaded[r % 2], 16 * (r // 2 + 1))
                    if w == WO:
                        act.wait_ge(product_done, K * (number[(PROD, 1)] + 1))
                    act.copy(split_into[w][0][:, k, :], raw[r % 2][:]).then_inc(raw_hi_done, 1)
                if stage == "take":
                    n = arg
                    hi, _ = result_of(n)
                    act.wait_ge(product_done, n + 1)
                    if n >= 2:
                        act.wait_ge(product_lo, n - 1)
                    if is_score(n):
                        s = n - K * number[(SCORE, 0)]
                        act.wait_ge(smax_done, s + 1)
                        act.mul(sbias[:, s:s + 1], smax[:, s:s + 1], -SCALE).then_inc(sbias_done, 1)
                        act.wait_ge(sbias_done, s + 1)
                        act.activation(full[n % 2][:], product_bank(n)[:], ACT.Exp, bias=sbias[:, s:s + 1], scale=SCALE,
                                       accum_out=ssum[:, s:s + 1]).then_inc(product_taken, 1)
                    else:
                        if n == K * number[(FOLD, 1)]:
                            act.wait_ge(product_done, K * (number[(MIX, 1)] + 1))
                        act.copy(hi, as_result(n, product_bank(n))).then_inc(product_hi, 1)
                        act.copy(as_result(n, full[n % 2]), as_result(n, product_bank(n))).then_inc(product_taken, 1)
                if stage == "norm":
                    n, s = arg, arg - K * number[(SCORE, 0)]
                    act.wait_ge(srec_done, s + 1)
                    act.activation(full[n % 2][:], full[n % 2][:], ACT.Copy, scale=srec[:, s:s + 1]).then_inc(snorm_done, 1)
                    act.wait_ge(snorm_done, s + 1)
                    act.copy(result_of(n)[0], full[n % 2][:]).then_inc(product_hi, 1)
                if stage == "mirror":
                    hi, lo = mat_x[arg]
                    turned = bank[4 * arg:4 * arg + 3]
                    act.wait_ge(mirrored, arg + 1)
                    for whole, half in zip(turned, (hi, lo)):
                        act.copy(half[:, 2:K, 0:2 * P], whole[:].rearrange("p (k d) -> p k d", k=2))
                    act.copy(hi[:, 1, 0:P], turned[2][:, 0:P])
                    act.copy(lo[:, 1, 0:P], turned[2][:, P:2 * P]).then_inc(mirror_taken, 1)
                if stage == "look":
                    make_leaves(arg)
                if stage == "built":
                    weight_high(arg)
                if stage == "first":
                    turn_first(arg)

            def ffn(b):
                for c in range(C):
                    n = rows(c)
                    act.wait_ge(gate_done, b.count(C, c))
                    if not (b.first and c == 0):
                        act.wait_ge(h_done, b.count(C, c - 1))
                    act.activation(h_gate[0:n, :], bank[4][0:n, :], ACT.Silu).then_inc(silu_done, 1)
                    act.wait_ge(h_done, b.count(C, c))
                    if b.first and c == 0:
                        act.wait_ge(x2_turned, K)
                    if c >= 2:
                        act.wait_ge(down_done, b.count(C, c - 2))
                    elif not b.first:
                        act.wait_ge(down_done, b.count(C, -1))
                    act.copy(h_hi[c % 2][0:n, :], h_full[0:n, :]).then_inc(h_hi_done, 1)
                    if b.first:
                        for k in late_looks(c):
                            make_leaves(k)
                            for u in built_by(k):
                                weight_high(u)
                    for step in preparation(b, c):
                        if step == "ln1":
                            act.wait_ge(x2_turned, b.count(K, K - 1))
                            normalise(b.next(), xn, 0)
                        elif step == "ln2":
                            act.wait_ge(xt_turned, b.next().count(T, T - 1))
                            normalise(b.next(), xn, 1)
                        elif step[0] == "turn":
                            x_high(b.next(), step[1])
                if not b.last:
                    x2_high(b.next())

            ffn(Block(0, 0))
            every_block(act, ffn)

        @blk.tensor
        def _(pe):
            def products(out_, terms):
                last = None
                for i, ((lh, ll), (rh, rl)) in enumerate(terms):
                    for j, (a, b) in enumerate(((lh, rh), (ll, rh), (lh, rl))):
                        last = pe.matmul(out_, a, b, start=(i == 0 and j == 0), stop=(i == len(terms) - 1 and j == 2))
                return last

            def turn_x(b, source, t):
                pe.wait_ge(ln1_done, b.count(T, t))
                if b.first and t == 0:
                    pe.wait_ge(product_taken, K * (number[(FOLD, 0)] + 1))
                elif t == 0:
                    pe.wait_ge(x2_lo_done, b.count(K, -1))
                elif b.between and t == 1:
                    pe.wait_ge(silu_done, C)
                else:
                    pe.wait_ge(xt_lo_done, b.count(T, t - (2 if b.between else 1)))
                for k in range(K):
                    last = pe.transpose(b.turn_bank(t)[:, k * P:(k + 1) * P], source[:, t, k * P:(k + 1) * P], ident[:])
                last.then_inc(xt_turned, 1)

            def attend(b, t):
                pe.wait_ge(xt_lo_done, b.count(T, t))
                if b.first and t == 0:
                    pe.wait_ge(product_lo, K * (number[(FOLD, 0)] + 1))
                if t:
                    pe.wait_ge(x1_done, b.count(T, t - 1))
                if not (isinstance(b.n, int) and b.n < 2):
                    pe.wait_ge(m_loaded, 32 * b.half)
                hi, lo = xt_hi[b.xt(t)], xt_lo[b.xt(t)]
                products(bank[7][:], [((hi[:, k, :], lo[:, k, :]), (m_hi[:, k, :], m_lo[:, k, :]))
                                      for k in range(K)]).then_inc(attn_done, 1)

            def turn_x2(b, source, k):
                if k == 0:
                    pe.wait_ge(ln2_done, b.count(T, T - 1))
                if k >= 2:
                    pe.wait_ge(x2_lo_done, b.count(K, k - 2))
                for t in range(T):
                    last = pe.transpose(bank[6 + k % 2][:, t * P:(t + 1) * P], source[:, t, k * P:(k + 1) * P], ident[:])
                last.then_inc(x2_turned, 1)

            operands = {PROD: (mat_x, wa), SCORE: (wb, mat_y), MIX: (mat_x, wa), FOLD: (wb, mat_y)}
            before = {PROD: GRAM, SCORE: PROD, MIX: SCORE, FOLD: MIX}
            weight = {PROD: WK, SCORE: WQ, MIX: WO}
            pe.wait_ge(const_made, 4)
            for stage, arg in timeline:
                if stage == "idx":
                    u, c, kind = arg, arg // 3, arg % 3
                    n = rows(c)
                    pe.wait_ge(idx_cast, u + 1)
                    if u >= 4:
                        pe.wait_ge(idx_laid, u - 3)
                    if u == U_HIGH_BANKS:
                        pe.wait_ge(product_taken, K)
                    if u == U_BEFORE_MIRROR:
                        pe.wait_ge(mirror_taken, 1)
                    turned = idx_bank(u)
                    for k in range(K):
                        if kind < 2:
                            last = pe.transpose(turned[:, k * P:k * P + n], idx_bf[u % 4][0:n, k * P:(k + 1) * P], ident_bf[0:n, 0:n])
                        else:
                            last = pe.transpose(turned[0:n, k * P:(k + 1) * P], idx_bf[u % 4][:, k * P:k * P + n], ident_bf[:])
                    last.then_inc(idx_turned, 1)
                if stage == "gram":
                    i, batch = arg, arg // (T * GB)
                    if i == T * GB:
                        pe.wait_ge(idx_laid, U_HIGH_BANKS)
                    pe.wait_ge(xg_lo_done, i + 1)
                    start, stop = i % (T * GB) == 0, i % (T * GB) == T * GB - 1
                    hi, lo = xg_hi[i % 4], xg_lo[i % 4]
                    for m in range(K):
                        rows_of, cols = slice(m * P, (m + 1) * P), slice(gram_first(m), D)
                        for j, (a, b) in enumerate(((hi, hi), (lo, hi), (hi, lo))):
                            last = pe.matmul(bank[4 * batch + m][:, cols], a[:, rows_of], b[:, cols],
                                             start=start and j == 0, stop=stop and j == 2)
                        if stop:
                            last.then_inc(product_done, 1)
                    if not stop:
                        last.then_inc(xg_used, 1)
                    elif i + 4 < T * NG:
                        pe.wait_ge(product_done, K * (batch + 1))
                        pe.sem_inc(xg_used, 1)
                if stage == "mirror":
                    b = arg
                    pe.wait_ge(product_lo, K * (b + 1))
                    pe.wait_ge(product_taken, K * (b + 1))
                    if b == 0:
                        pe.wait_ge(idx_laid, U_BEFORE_MIRROR)
                    pairs = [(0, 2), (1, 2), (0, 3), (1, 3)]
                    for i, half in enumerate(mat_x[b]):
                        source = half[:].bitcast(F32)
                        for j, (row, col) in enumerate(pairs):
                            pe.transpose(bank[4 * b + i][:, j * P:(j + 1) * P], source[:, row, col * P:(col + 1) * P], ident[:])
                        last = pe.transpose(bank[4 * b + 2][:, i * P:(i + 1) * P], source[:, 0, P:2 * P], ident[:])
                    last.then_inc(mirrored, 1)
                if stage == "product":
                    n = arg
                    (name, b), m = groups[n // K], n % K
                    if name == PROD and m == 0:
                        pe.wait_ge(mirror_taken, b + 1)
                        if b == 0:
                            pe.wait_ge(idx_laid, U)
                    pe.wait_ge(product_taken, n - 2 * K + 1)
                    if name == TURN_V:
                        r = K * WV + m
                        pe.wait_ge(raw_loaded[r % 2], 16 * (r // 2 + 1))
                        for k in range(K):
                            last = pe.transpose(product_bank(n)[:, k * P:(k + 1) * P], raw[r % 2][:, k * P:(k + 1) * P], ident[:])
                        last.then_inc(product_done, 1)
                        continue
                    left, right = operands[name]
                    left = left[b] if name in (PROD, MIX) else left
                    right = right if name in (PROD, MIX) else right[b]
                    pe.wait_ge(product_lo, K * (number[(before[name], b)] + 1))
                    if name in weight:
                        pe.wait_ge(raw_lo_done, K * (weight[name] + 1))
                    else:
                        pe.wait_ge(product_lo, K * (number[(TURN_V, 0)] + 1))
                    products(product_bank(n)[:], [([a[:, k, m * P:(m + 1) * P] for a in left], [a[:, k, :] for a in right])
                                                  for k in range(K)]).then_inc(product_done, 1)
                if stage == "first":
                    if arg == "x2":
                        for k in range(K):
                            turn_x2(Block(0, 0), xn_first, k)
                    elif arg[0] == "turn":
                        turn_x(Block(0, 0), xn_first, arg[1])
                    elif arg[0] == "attend":
                        attend(Block(0, 0), arg[1])

            def ffn(b):
                def down(c):
                    n = rows(c)
                    pe.wait_ge(h_lo_done, b.count(C, c))
                    if c == 0 and not b.first:
                        pe.wait_ge(y_added, b.count(T, -1))
                    if b.first:
                        pe.wait_ge(w_lo_done, 3 * c + 3)
                        if c == 0:
                            pe.wait_ge(product_taken, LAST_ITEM)
                    for t in range(T):
                        tokens = slice(t * P, (t + 1) * P)
                        hi, lo = h_hi[c % 2][0:n, tokens], h_lo[c % 2][0:n, tokens]
                        w = w_hi[c][0:n, 2, :], w_lo[c][0:n, 2, :]
                        for j, (a, x) in enumerate(((hi, w[0]), (lo, w[0]), (hi, w[1]))):
                            last = pe.matmul(bank[t][:], a, x, start=(c == 0 and j == 0), stop=(c == C - 1 and j == 2))
                    last.then_inc(down_done, 1)

                for c in range(C):
                    n = rows(c)
                    if c == 0:
                        pe.wait_ge(x2_lo_done, b.count(K, K - 1))
                    for kind, done, read in ((0, gate_done, silu_done), (1, up_done, h_done)):
                        if b.first:
                            pe.wait_ge(w_lo_done, 3 * c + kind + 1)
                        if not (b.first and c == 0):
                            pe.wait_ge(read, b.count(C, c - 1))
                        products(bank[4 + kind][0:n, :],
                                 [([w[c][:, kind, k * P:k * P + n] for w in (w_hi, w_lo)], (x2t_hi[:, k, :], x2t_lo[:, k, :]))
                                  for k in range(K)]).then_inc(done, 1)
                    for step in preparation(b, c):
                        if step[0] == "turn":
                            turn_x(b.next(), xn, step[1])
                        elif step[0] == "attend":
                            attend(b.next(), step[1])
                        elif step == "down":
                            down(c - 1)
                        elif step == "last down":
                            down(c)
                    if c == C - 1 and not b.last:
                        turn_x2(b.next(), xn, 0)
                        turn_x2(b.next(), xn, 1)
                    if c and not (b.first and c == C - 1):
                        down(c - 1)
                if not b.last:
                    turn_x2(b.next(), xn, 2)
                    turn_x2(b.next(), xn, 3)
                if not b.first:
                    down(C - 1)

            ffn(Block(0, 0))
            every_block(pe, ffn)

        @blk.vector
        def _(dve):
            class Steps:
                base, n = 0, 0

            def step(ins):
                Steps.n += 1
                ins.then_inc(dve_steps, 1)
                return Steps.base + Steps.n

            def need(value):
                dve.wait_ge(dve_steps, value)

            def norm_stats(x, which, done):
                for t in range(T):
                    last = dve.bn_stats(bn[:, t, :], x[:, t, :])
                need(step(last))
                dve.memset(tmp[:], 0.0)
                for t in range(T):
                    last = dve.bn_aggr(mv[:, t, :], bn[:, t, :])
                need(step(last))
                need(step(dve.tensor_scalar(var[:], mv[:, :, 1], EPS, None, ALU.add)))
                y = rstd[which]
                need(step(dve.tensor_scalar(y[:].bitcast(I32), var[:].bitcast(I32), -0.5, RSQRT_SEED, ALU.mult, ALU.add)))
                for _ in range(NEWTON):
                    need(step(dve.tensor_tensor(tmp[:], y[:], y[:], ALU.mult)))
                    need(step(dve.scalar_tensor_tensor(out=tmp[:], in0=tmp[:], scalar=-0.5, in1=var[:], op0=ALU.mult, op1=ALU.mult)))
                    need(step(dve.scalar_tensor_tensor(out=y[:], in0=tmp[:], scalar=1.5, in1=y[:], op0=ALU.add, op1=ALU.mult)))
                dve.scalar_tensor_tensor(out=shift[which][:], in0=mv[:, :, 0], scalar=-1.0, in1=y[:], op0=ALU.mult,
                                         op1=ALU.mult).then_inc(done, 1)

            STEPS_PER_NORM = 4 + 3 * NEWTON

            def merge(bit, keep, other):
                return dve.copy_predicated(keep[:], bit_mask[bit][:], other[:])

            def pairs_of(byte):
                return byte * 257

            def find_bit(u, bit):
                return step(dve.tensor_scalar(bit_mask[bit][:].bitcast(I16), idx_in[u % 3][:].bitcast(I16), pairs_of(1 << bit),
                                              None, ALU.bitwise_and))

            def find_high(u):
                dve.wait_ge(idx_back[u % 3], 16 * (u // 3 + 1))
                if u >= 2:
                    dve.wait_ge(leaf_made, leaf_count(u - 2, 6))
                dve.tensor_scalar(high_bit[u % 2][:].bitcast(I16), idx_in[u % 3][:].bitcast(I16), HIGH_BIT, pairs_of(1),
                                  ALU.logical_shift_right, ALU.bitwise_and).then_inc(high_made, 1)

            def leaf_0(u):
                dve.wait_ge(high_made, u + 1)
                if u >= 2:
                    dve.wait_ge(w_lo_done, u - 1)
                return step(dve.tensor_scalar(picked[u % 2][:], high_bit[u % 2][:], lut_step[:, 0:1], lut[:, 0:1],
                                              ALU.mult, ALU.add))

            def look_up():
                x, y, z, w, v = part
                find_high(0)
                leaf_0(0)
                for bit in range(3):
                    ready = find_bit(0, bit)
                for u in range(U):
                    r, more = picked[u % 2], u + 1 < U
                    need(ready)
                    dve.wait_ge(leaf_made, leaf_count(u, 3))
                    merge(0, y, z).then_inc(merged, 1)
                    yield
                    dve.wait_ge(leaf_made, leaf_count(u, 1))
                    merge(0, r, x).then_inc(merged, 1)
                    yield
                    dve.wait_ge(leaf_made, leaf_count(u, 4))
                    merge(0, w, v).then_inc(merged, 1)
                    yield
                    dve.wait_ge(merged, merge_count(u, M_RX))
                    merge(1, r, y).then_inc(merged, 1)
                    yield
                    dve.wait_ge(leaf_made, leaf_count(u, 6))
                    merge(0, x, z).then_inc(merged, 1)
                    yield
                    if more:
                        find_high(u + 1)
                    yield
                    dve.wait_ge(merged, merge_count(u, M_XZ))
                    merge(1, w, x).then_inc(merged, 1)
                    yield
                    if more:
                        find_bit(u + 1, 0)
                    yield
                    if more:
                        leaf_0(u + 1)
                    yield
                    dve.wait_ge(merged, merge_count(u, M_WX))
                    merge(2, r, w).then_inc(picked_done, 1)
                    yield
                    if more:
                        find_bit(u + 1, 1)
                    yield
                    if more:
                        dve.wait_ge(picked_done, u + 1)
                        ready = find_bit(u + 1, 2)
                    yield

            def x_low(b, t):
                dve.wait_ge(xt_hi_done, b.count(T, t))
                hi, lo = (a[b.xt(t)][:].rearrange("p k s -> p (k s)") for a in (xt_hi, xt_lo))
                dve.tensor_tensor(lo, b.turn_bank(t)[:], hi.bitcast(F32), ALU.subtract).then_inc(xt_lo_done, 1)

            def add_attention(b, t):
                dve.wait_ge(attn_done, b.count(T, t))
                dve.wait_ge(ln1_done, b.count(T, t))
                dve.tensor_tensor(x1[b.parity][:, t, :], bank[7][:], x1[b.parity][:, t, :], ALU.add).then_inc(x1_done, 1)

            def x2_low(b):
                for k in range(K):
                    dve.wait_ge(x2_hi_done, b.count(K, k))
                    dve.tensor_tensor(x2t_lo[:, k, :], bank[6 + k % 2][:], x2t_hi[:, k, :].bitcast(F32),
                                      ALU.subtract).then_inc(x2_lo_done, 1)

            def stats1(b):
                dve.wait_ge(x_loaded[b.parity], 16 * (b.half + 1))
                if not b.first:
                    dve.wait_ge(ln1_done, b.count(T, -1))
                norm_stats(x1[b.parity], 0, ln1_stats)

            def stats2(b):
                dve.wait_ge(x1_done, b.count(T, T - 1))
                if not b.first:
                    dve.wait_ge(ln2_done, b.count(T, -1))
                norm_stats(x1[b.parity], 1, ln2_stats)

            first = Block(0, 0)
            looks = look_up()
            dve.wait_ge(lut_loaded, 16)
            dve.tensor_tensor(lut_step[:], lut[:, HALF:LUT], lut[:, 0:HALF], ALU.subtract).then_inc(step_made, 1)
            dve.wait_ge(step_made, 1)
            for stage, arg in timeline:
                if stage == "cast":
                    u, c, kind = arg, arg // 3, arg % 3
                    n = rows(c)
                    dve.wait_ge(idx_loaded[u % 8], 16 * (u // 8 + 1))
                    if u >= 4:
                        dve.wait_ge(idx_turned, u - 3)
                    src, dst = idx_raw[u % 8][:, :], idx_bf[u % 4][:, :]
                    if kind < 2:
                        src, dst = src[0:n, :], dst[0:n, :]
                    else:
                        src, dst = (a.rearrange("p (k i) -> p k i", k=K)[:, :, 0:n] for a in (src, dst))
                    dve.tensor_copy(dst, src).then_inc(idx_cast, 1)
                if stage == "stats":
                    g = arg
                    dve.wait_ge(xg_loaded[g % 3], 16 * (g // 3 + 1))
                    if g >= 2:
                        dve.wait_ge(xg_normed, T * (g - 1))
                    norm_stats(xg[g % 3], g % 2, xg_stats)
                if stage == "take" and is_score(arg):
                    s = arg - K * number[(SCORE, 0)]
                    dve.wait_ge(product_done, arg + 1)
                    dve.reduce_max(smax[:, s:s + 1], product_bank(arg)[:], AX_X).then_inc(smax_done, 1)
                if stage == "norm":
                    s = arg - K * number[(SCORE, 0)]
                    dve.wait_ge(product_taken, arg + 1)
                    dve.reciprocal(srec[:, s:s + 1], ssum[:, s:s + 1]).then_inc(srec_done, 1)
                if stage == "look":
                    next(looks)
                if stage == "first":
                    if arg == "stats1":
                        dve.wait_ge(xg_normed, T * NG)
                        stats1(first)
                    elif arg == "stats2":
                        stats2(first)
                    elif arg == "x2":
                        x2_low(first)
                    elif arg[0] == "turn":
                        x_low(first, arg[1])
                    elif arg[0] == "attend":
                        add_attention(first, arg[1])

            def ffn(b):
                for c in range(C):
                    n = rows(c)
                    dve.wait_ge(up_done, b.count(C, c))
                    dve.wait_ge(silu_done, b.count(C, c))
                    if not (b.first and c == 0):
                        dve.wait_ge(h_lo_done, b.count(C, c - 1))
                    dve.tensor_tensor(h_full[0:n, :], bank[5][0:n, :], h_gate[0:n, :], ALU.mult).then_inc(h_done, 1)
                    if b.first:
                        for _ in late_looks(c):
                            next(looks)
                    for s in preparation(b, c):
                        if s == "stats1":
                            stats1(b.next())
                        elif s == "stats2":
                            stats2(b.next())
                        elif s[0] == "turn":
                            x_low(b.next(), s[1])
                        elif s[0] == "attend":
                            add_attention(b.next(), s[1])
                if not b.last:
                    x2_low(b.next())
                dve.wait_ge(down_done, b.count(C, C - 1))
                for t in range(T):
                    dve.tensor_tensor(x1[b.parity][:, t, :], bank[t][:], x1[b.parity][:, t, :], ALU.add).then_inc(y_added, 1)

            ffn(first)
            begun, pairs = Steps.n, (NG - 2) // 2
            with dve.Fori(0, pairs) as j:
                Steps.base, Steps.n = 4 * STEPS_PER_NORM * j, begun
                ffn(Block(j, 1))
                ffn(Block(j, 2))
            assert Steps.n == begun + 4 * STEPS_PER_NORM
            Steps.base, Steps.n = 0, begun + 4 * STEPS_PER_NORM * pairs
            ffn(Block(0, NG - 1))


_INS = ["L0_attn_x", "L0_attn_Wq", "L0_attn_Wk", "L0_attn_Wv", "L0_attn_Wo", "L0_ffn_lut", "L0_ffn_gate_idx",
        "L0_ffn_up_idx", "L0_ffn_down_idx"]
_ARGS = ["x_in", "wq_in", "wk_in", "wv_in", "wo_in", "lut_in", "gate_in", "up_in", "down_in"]


def kernel(**inputs):
    import numpy as _np
    import concourse.bacc as _bacc
    from concourse import mybir as _mybir
    from concourse.bass_utils import run_bass_kernel_spmd as _run

    nc = _bacc.Bacc("TRN2", target_bir_lowering=False, num_devices=1)
    arrays, args = {}, {}
    for name, arg in zip(_INS, _ARGS):
        a = _np.ascontiguousarray(inputs[name])
        arrays[f"in_{name}"] = a
        args[arg] = nc.dram_tensor(f"in_{name}", a.shape, _mybir.dt.from_np(a.dtype), kind="ExternalInput").ap()
    shape = arrays["in_L0_attn_x"].shape
    out = nc.dram_tensor("out_dram", shape, _mybir.dt.float32, kind="ExternalOutput").ap()
    preln_attention_ghost_ffn(nc, out=out, **args)
    r = _run(nc, [arrays], core_ids=[0])
    return r.results[0]["out_dram"]
```

```python
from contextlib import ExitStack

import concourse.bass as bass
from concourse import mybir
from concourse.alu_op_type import AluOpType as ALU

ACT = mybir.ActivationFunctionType
AX_X = mybir.AxisListType.X
F32 = mybir.dt.float32
F32R = mybir.dt.float32r
BF16 = mybir.dt.bfloat16
I16 = mybir.dt.int16
I32 = mybir.dt.int32
U8 = mybir.dt.uint8

P = 128
EPS = 1e-5
RSQRT_SEED = float(0x5F3759DF)
NEWTON = 3
NORM_PIECES = 5 + 3 * NEWTON
KIB = 1024


def preln_attention_ghost_ffn(nc, x_in, wq_in, wk_in, wv_in, wo_in, lut_in, gate_in, up_in, down_in, out):
    B, S, D = x_in.shape
    I = gate_in.shape[0]
    LUT = lut_in.shape[0]
    K = D // P
    T = 4
    BT = T * P
    NG = B * S // BT
    GB = S // BT
    C = -(-I // P)
    HALF = LUT // 2
    HIGH_BIT = 3
    SCALE = 1.0 / float((D // 32) ** 0.5)

    def rows(c):
        return min(P, I - c * P)

    U = 3 * C
    LOOKS_GRAM, LOOKS_CHAIN = 2, 3
    LOOKS_TAKE, MIRROR_ITEM = 2, 2
    LOOKS_NORM, LOOKS_SCORE = 3, 0
    LOOKS_STATS = 4
    FIRST_LOOK = 8
    LATE_SLOTS = 9
    LOOKS_FIRST = 8, 8, 8, 8
    assert (D, K, C, NG, GB, LUT) == (512, 4, 11, 8, 4, 16)

    xb_dram = x_in.rearrange("b s d -> (b s) d").rearrange("(n p t) d -> n p t d", p=P, t=T)
    ob_dram = out.rearrange("b s d -> (b s) d").rearrange("(n p t) d -> n p t d", p=P, t=T)

    ctx = ExitStack()
    with ctx:
        base = 16512

        def at(name, kib, shape, dt):
            return nc.alloc_sbuf_tensor_at(name, shape, dt, offset=base + int(kib * KIB))

        def sem(name):
            return ctx.enter_context(nc.semaphore(name))

        w_at = [12 * c + (8 if c >= 8 else 0) for c in range(C)]
        w_hi = [at(f"w_hi{c}", w_at[c], [P, 3, D], F32R) for c in range(C)]
        w_lo = [at(f"w_lo{c}", w_at[c] + 6, [P, 3, D], F32R) for c in range(C)]
        x2t_hi = at("x2t_hi", 140, [P, K, BT], F32R)
        x2t_lo = at("x2t_lo", 148, [P, K, BT], F32R)
        m_hi = at("m_hi", 156, [P, K, D], F32R)
        m_lo = at("m_lo", 164, [P, K, D], F32R)
        x1 = [at("x1a", 96, [P, T, D], F32), at("x1b", 188, [P, T, D], F32)]
        h_hi = [at(f"h_hi{i}", 172 + 4 * i, [P, BT], F32R) for i in range(2)]
        h_lo = [at(f"h_lo{i}", 174 + 4 * i, [P, BT], F32R) for i in range(2)]
        h_gate = at("h_gate", 180, [P, BT], F32)
        h_full = at("h_full", 182, [P, BT], F32)
        xt_hi = [at(f"xt_hi{i}", 184 - 4 * i, [P, K, P], F32R) for i in range(2)]
        xt_lo = [at(f"xt_lo{i}", 186 - 4 * i, [P, K, P], F32R) for i in range(2)]
        xn = at("xn", 196, [P, T, D], F32)
        xn_first = at("xn_first", 172, [P, T, D], F32)
        mat_x = [(at(f"mat_x_hi{b}", 60 + 32 * b, [P, K, D], F32R), at(f"mat_x_lo{b}", 68 + 32 * b, [P, K, D], F32R)) for b in range(B)]
        mat_y = [(at(f"mat_y_hi{b}", 76 + 32 * b, [P, K, D], F32R), at(f"mat_y_lo{b}", 84 + 32 * b, [P, K, D], F32R)) for b in range(B)]
        wa = (at("wa_hi", 132, [P, K, D], F32R), at("wa_lo", 140, [P, K, D], F32R))
        wb = (at("wb_hi", 148, [P, K, D], F32R), at("wb_lo", 124, [P, K, D], F32R))
        raw = [at(f"raw{i}", 184 + 2 * i, [P, D], F32) for i in range(2)]
        full = [at(f"full{i}", 180 + 2 * i, [P, D], F32) for i in range(2)]
        xg = [at(f"xg{i}", kib, [P, T, D], F32) for i, kib in enumerate((76, 84, 156))]
        xg_hi = [at(f"xg_hi{i}", 108 + 4 * i, [P, D], F32R) for i in range(4)]
        xg_lo = [at(f"xg_lo{i}", 110 + 4 * i, [P, D], F32R) for i in range(4)]
        xg_n = [at(f"xg_n{i}", 164 + 2 * i, [P, D], F32) for i in range(4)]
        idx_raw = [at(f"idx_raw{i}", 92 + 2 * i, [P, D], I32) for i in range(8)]
        idx_bf = [at(f"idx_bf{i}", 172 + 1 * i, [P, D], BF16) for i in range(4)]
        idx_out = [at(f"idx_out{i}", 176 + i / 2, [P, D], U8) for i in range(4)]
        picked = [at("picked0", 188, [P, D], F32), at("picked1", 190, [P, D], F32)]
        part = [at(f"part{i}", kib, [P, D], F32) for i, kib in enumerate((192, 194, 196, 198, 205.75))]
        high_bit = [at(f"high_bit{i}", 203 + i / 2, [P, D], U8) for i in range(2)]
        bit_mask = [at(f"bit_mask{i}", 200 + i / 2, [P, D], U8) for i in range(3)]
        idx_in = [at(f"idx_in{i}", 201.5 + i / 2, [P, D], U8) for i in range(3)]
        ident = at("ident", 204, [P, P], F32)
        ident_bf = at("ident_bf", 204.5, [P, P], BF16)
        lut = at("lut", 204.75, [P, LUT], F32)
        lut_step = at("lut_step", 204.8125, [P, HALF], F32)
        bn = at("bn", 204.875, [P, T, 6], F32)
        mv = at("mv", 205, [P, T, 2], F32)
        var = at("var", 205.0625, [P, T], F32)
        tmp = at("tmp", 205.125, [P, T], F32)
        rstd = [at(f"rstd{i}", 205.1875 + i / 32, [P, T], F32) for i in range(2)]
        shift = [at(f"shift{i}", 205.25 + i / 32, [P, T], F32) for i in range(2)]
        rstd_kept = [at(f"rstd_kept{i}", 205.3125 + i / 32, [P, T], F32) for i in range(2)]
        shift_kept = [at(f"shift_kept{i}", 205.375 + i / 32, [P, T], F32) for i in range(2)]
        smax = at("smax", 205.4375, [P, 2 * K], F32)
        sbias = at("sbias", 205.5, [P, 2 * K], F32)
        ssum = at("ssum", 205.5625, [P, 2 * K], F32)
        srec = at("srec", 205.625, [P, 2 * K], F32)

        bank = [ctx.enter_context(nc.psum_tensor(f"bank{i}", [P, D], F32)) for i in range(8)]
        idx_dram = nc.dram_tensor("idx_scratch", (U, P, D), U8).ap()
        m_dram = nc.dram_tensor("m_scratch", (B, 2, P, K * D), F32).ap()

        const_made = sem("const_made")
        lut_loaded = sem("lut_loaded")
        dve_steps = sem("dve_steps")
        idx_loaded = [sem(f"idx_loaded{i}") for i in range(8)]
        idx_cast = sem("idx_cast")
        idx_turned = sem("idx_turned")
        idx_laid = sem("idx_laid")
        idx_stored = [sem(f"idx_stored{i}") for i in range(4)]
        idx_back = [sem(f"idx_back{i}") for i in range(3)]
        step_made = sem("step_made")
        high_made = sem("high_made")
        leaf_made = sem("leaf_made")
        pool_leaf_made = sem("pool_leaf_made")
        merged = sem("merged")
        idx_cleared = sem("idx_cleared")
        mirrored = sem("mirrored")
        mirror_taken = sem("mirror_taken")
        picked_done = sem("picked_done")
        w_hi_done = sem("w_hi_done")
        w_lo_done = sem("w_lo_done")
        xg_loaded = [sem(f"xg_loaded{i}") for i in range(3)]
        xg_stats = sem("xg_stats")
        xg_normed = sem("xg_normed")
        xg_hi_done = sem("xg_hi_done")
        xg_lo_done = sem("xg_lo_done")
        xg_used = sem("xg_used")
        raw_loaded = [sem(f"raw_loaded{i}") for i in range(2)]
        raw_hi_done = sem("raw_hi_done")
        raw_lo_done = sem("raw_lo_done")
        product_done = sem("product_done")
        product_hi = sem("product_hi")
        product_lo = sem("product_lo")
        smax_done = sem("smax_done")
        sbias_done = sem("sbias_done")
        sexp_done = sem("sexp_done")
        srec_done = sem("srec_done")
        m_stored = sem("m_stored")
        m_loaded = sem("m_loaded")
        x_loaded = [sem(f"x_loaded{i}") for i in range(2)]
        out_stored = [sem(f"out_stored{i}") for i in range(2)]
        ln1_stats = sem("ln1_stats")
        ln1_done = sem("ln1_done")
        xt_turned = sem("xt_turned")
        xt_hi_done = sem("xt_hi_done")
        xt_lo_done = sem("xt_lo_done")
        attn_done = sem("attn_done")
        x1_done = sem("x1_done")
        ln2_stats = sem("ln2_stats")
        ln2_done = sem("ln2_done")
        x2_turned = sem("x2_turned")
        x2_hi_done = sem("x2_hi_done")
        x2_lo_done = sem("x2_lo_done")
        gate_done = sem("gate_done")
        up_done = sem("up_done")
        silu_done = sem("silu_done")
        h_done = sem("h_done")
        h_hi_done = sem("h_hi_done")
        h_lo_done = sem("h_lo_done")
        down_done = sem("down_done")
        y_added = sem("y_added")

        GRAM, PROD, SCORE, TURN_V, MIX, FOLD = "gram", "prod", "score", "turn_v", "mix", "fold"
        groups = [(GRAM, 0), (GRAM, 1), (PROD, 0), (PROD, 1), (SCORE, 0), (SCORE, 1),
                  (TURN_V, 0), (MIX, 0), (MIX, 1), (FOLD, 0), (FOLD, 1)]
        number = {g: q for q, g in enumerate(groups)}
        LAST_ITEM = K * len(groups)
        WK, WQ, WO, WV = range(4)
        raws = [wk_in, wq_in, wo_in, wv_in]
        split_into = {WK: wa, WQ: wb, WO: wa}

        def product_bank(n):
            return bank[4 * (n // K % 2) + n % K]

        def result_of(n):
            (name, b), m = groups[n // K], n % K
            if name == TURN_V:
                return [a[:, :, m * P:(m + 1) * P] for a in wb]
            pair = {GRAM: mat_x[b], SCORE: mat_x[b], PROD: mat_y[b], MIX: mat_y[b],
                    FOLD: (m_hi, m_lo) if b == 0 else wa}[name]
            first = gram_first(m) if name == GRAM else 0
            return [a[:, m, first:] for a in pair]

        def as_result(n, tile):
            name, m = groups[n // K][0], n % K
            if name == TURN_V:
                return tile[:].rearrange("p (k d) -> p k d", k=K)
            return tile[:, gram_first(m):] if name == GRAM else tile[:]

        def gram_first(m):
            return P * min(m, K - 2)

        def is_score(n):
            return groups[n // K][0] == SCORE

        LAG = 2
        OPS = 11
        LEAVES = [2, 3, 1, 7, 6]
        POOL_LEAVES = [0, 5, 4]
        LEAVES_NEXT = {4: [0], 5: [2, 3], 6: [1, 5], 8: [4]}
        LEAVES_SAME = {0: [7], 1: [6]}
        tile_of_leaf = {1: 0, 2: 1, 3: 2, 4: 3, 5: 4, 6: 0, 7: 2}
        M_YZ, M_RX, M_WV, M_RY, M_XZ, M_WX = range(6)
        MERGES = 6

        def merge_count(u, which):
            return MERGES * u + which + 1

        def leaf_count(u, j):
            return len(LEAVES) * u + LEAVES.index(j) + 1

        def pool_leaf_count(u, j):
            return len(POOL_LEAVES) * u + POOL_LEAVES.index(j) + 1

        def leaves_at(k, mine):
            if k == 0:
                return [(0, j) for j in LEAVES[0:3] + POOL_LEAVES if j in mine]
            if k < LAG:
                return []
            u, p = divmod(k - LAG, OPS)
            both = [(u, j) for j in LEAVES_SAME.get(p, [])] + [(u + 1, j) for j in LEAVES_NEXT.get(p, [])]
            return [(v, j) for v, j in both if j in mine and v < U]

        def make_leaf(eng, u, j):
            eng.wait_ge(high_made, u + 1)
            if u and j in (1, 2, 3, 5):
                eng.wait_ge(merged, merge_count(u - 1, {1: M_WX, 2: M_RY, 3: M_XZ, 5: M_WV}[j]))
            if u and j == 4:
                eng.wait_ge(picked_done, u)
            if j in (6, 7):
                eng.wait_ge(merged, merge_count(u, {6: M_RX, 7: M_YZ}[j]))
            if j == 0 and u >= 2:
                eng.wait_ge(w_lo_done, u - 1)
            tile = part[tile_of_leaf[j]] if j else picked[u % 2]
            return tile[:], high_bit[u % 2][:], lut_step[:, j:j + 1], lut[:, j:j + 1]

        timeline = []
        looked = [0]

        def look(n, limit):
            for _ in range(min(n, OPS * limit - looked[0])):
                timeline.append(("look", looked[0]))
                looked[0] += 1
                if looked[0] % OPS == 0:
                    timeline.append(("built", looked[0] // OPS - 1))

        def stats(entry, n, limit):
            timeline.append(entry)
            for piece in range(1, NORM_PIECES):
                look(n * piece // (NORM_PIECES - 1) - n * (piece - 1) // (NORM_PIECES - 1), limit)
                timeline.append(("stats_go_on", None))

        def normalised(n, limit):
            timeline.append(("norm", n))
            look(LOOKS_NORM, limit)
            timeline.append(("norm_low", n))

        def room(n):
            return 15 if n < K * (number[(MIX, 0)] + 1) else 18 if n < K * (number[(FOLD, 0)] + 1) else 24

        idx_per_tile = [1 + (i % 4 == 3) if i < T * GB else (i >= T * GB + 4) + (i == T * NG - 1) for i in range(T * NG)]
        assert sum(idx_per_tile) == U
        MIRROR_AT = T * NG - 4
        U_HIGH_BANKS = sum(idx_per_tile[0:T * GB])
        U_BEFORE_MIRROR = sum(idx_per_tile[0:MIRROR_AT])
        AHEAD = 2
        timeline += [("cast", u) for u in range(3)]
        stats(("stats", 0), 0, 0)
        timeline += [("gram_n", i) for i in range(AHEAD + 1)] + [("gram_in", i) for i in range(AHEAD)]
        u = 0
        for i in range(T * NG):
            if i % T == 0 and i // T + 1 < NG:
                stats(("stats", i // T + 1), LOOKS_STATS if i >= FIRST_LOOK else 0, 15)
            if i + AHEAD + 1 < T * NG:
                timeline.append(("gram_n", i + AHEAD + 1))
            if i + AHEAD < T * NG:
                timeline.append(("gram_in", i + AHEAD))
            for _ in range(idx_per_tile[i]):
                timeline += ([("cast", u + 3)] if u + 3 < U else []) + [("idx", u)]
                u += 1
            timeline.append(("gram", i))
            if T * GB <= i < T * GB + K:
                timeline.append(("take", i - T * GB))
            if 12 <= i < 28 and i % 2 == 0:
                timeline.append(("raw", divmod((i - 12) // 2, K)))
            if i == MIRROR_AT - 1:
                timeline.append(("mirror", 0))
            look(LOOKS_GRAM if i >= FIRST_LOOK else 0, 15)
        for n in range(K, LAST_ITEM):
            if n == K * number[(PROD, 0)] + MIRROR_ITEM:
                timeline.append(("mirror", 1))
            if n >= 2 * K:
                timeline.append(("product", n))
            if n == K * number[(FOLD, 1)]:
                timeline.append(("first", "ln1"))
            timeline.append(("take", n))
            if is_score(n):
                if is_score(n - 1):
                    normalised(n - 1, room(n))
                if not is_score(n + 1):
                    normalised(n, room(n))
                if n < K * (number[(SCORE, 0)] + 1):
                    timeline.append(("raw", (WO, n % K)))
            if groups[n // K] == (FOLD, 1):
                t = n % K
                timeline += ([("first", ("attend", t - 1))] if t else []) + [("first", ("turn", t))]
                look(LOOKS_FIRST[0], room(n))
            else:
                look(LOOKS_TAKE if n < 2 * K else LOOKS_SCORE if is_score(n) else LOOKS_CHAIN, room(n))
        look(LOOKS_FIRST[1], room(n))
        timeline.append(("first", ("attend", T - 1)))
        stats(("first", "stats2"), LOOKS_FIRST[2], U)
        timeline.append(("first", "ln2"))
        look(LOOKS_FIRST[3], U)
        timeline.append(("first", "x2"))
        early = looked[0]

        def late_looks(b, c, half):
            if not b.first or c >= LATE_SLOTS:
                return range(0)
            n, i = OPS * U - early, 2 * c + half
            return range(early + n * i // (2 * LATE_SLOTS), early + n * (i + 1) // (2 * LATE_SLOTS))

        def built_by(k):
            return [k // OPS] if k % OPS == OPS - 1 else []

        def scale_of(g):
            return (rstd_kept[g], shift_kept[g]) if g < 2 else (rstd[g % 2], shift[g % 2])

        def idx_bank(u):
            return bank[(4 if u < U_HIGH_BANKS else 0) + u % 4][:].bitcast(BF16)

        class Block:

            def __init__(self, j, off):
                self.j, self.off = j, off
                fixed = isinstance(j, int)
                self.n = 2 * j + off
                self.first = fixed and self.n == 0
                self.last = fixed and self.n == NG - 1
                self.parity = off % 2
                self.half = j + off // 2
                self.between = fixed and self.n == 1
                self.exposed = fixed and self.n < 2

            def next(self):
                return None if self.last else Block(self.j, self.off + 1)

            def count(self, per, i):
                return per * self.n + (i + 1)

            def xt(self, t):
                return t % 2 if self.between else 0

            def turn_bank(self, t):
                return bank[(6, 4)[self.xt(t)]]

            def x2_bank(self, k):
                return bank[(6, 7, 4, 5)[k] if self.exposed else 6 + k % 2]

        for c in range(1, LATE_SLOTS):
            assert late_looks(Block(0, 0), c - 1, 1).stop >= 3 * OPS * (c + 1)

        LN1_STATS, LN1, TURN, LN2 = 1, 2, 3, 8

        def preparation(b, c):
            if b.last:
                return []
            if b.first:
                return ["ln1", ("turn", 0), ("turn", 1), "down", ("attend", 0), ("turn", 2), ("attend", 1), ("turn", 3),
                        ("attend", 2), "last down", ("attend", 3), "stats2", "ln2"] if c == C - 1 else []
            steps = {LN1_STATS: ["stats1"], LN1: ["ln1"], LN2: ["ln2"], TURN + T: [("attend", T - 1), "stats2"]}
            for t in range(T):
                if TURN + t <= c and c == TURN + t:
                    return ([("attend", t - 1)] if t else []) + [("turn", t)]
            return steps.get(c, [])

        def every_block(eng, run):
            with eng.Fori(0, (NG - 2) // 2) as j:
                run(Block(j, 1))
                run(Block(j, 2))
            run(Block(0, NG - 1))

        blk = ctx.enter_context(nc.Block())

        @blk.sync
        def _(sp):
            def load_idx(u):
                c, kind = u // 3, u % 3
                if u >= 8:
                    sp.wait_ge(idx_cast, u - 7)
                n = rows(c)
                if kind < 2:
                    src = (gate_in, up_in)[kind][c * P:c * P + n, :]
                    sp.dma_start(idx_raw[u % 8][0:n, :], src).then_inc(idx_loaded[u % 8], 16)
                else:
                    src = down_in[:, c * P:c * P + n].rearrange("(k p) i -> p k i", p=P)
                    dst = idx_raw[u % 8][:, :].rearrange("p (k i) -> p k i", k=K)[:, :, 0:n]
                    sp.dma_start(dst, src).then_inc(idx_loaded[u % 8], 16)

            def store_idx(u):
                sp.wait_ge(idx_laid, u + 1)
                sp.dma_start(idx_dram[u], idx_out[u % 4][:]).then_inc(idx_stored[u % 4], 16)

            def load_raw(w, k):
                r = K * w + k
                if r >= K * WV + 2:
                    sp.wait_ge(product_done, K * number[(TURN_V, 0)] + r - K * WV - 1)
                elif r >= 2:
                    sp.wait_ge(raw_lo_done, r - 1)
                sp.dma_start(raw[r % 2][:], raws[w][k * P:(k + 1) * P, :]).then_inc(raw_loaded[r % 2], 16)

            def load_gram(g):
                if g >= 3:
                    sp.wait_ge(xg_normed, T * (g - 2))
                sp.dma_start(xg[g % 3][:], xb_dram[g]).then_inc(xg_loaded[g % 3], 16)

            load_gram(0)
            for u in range(4):
                load_idx(u)
            load_gram(1)
            for u in range(4, 8):
                load_idx(u)
            load_gram(2)
            load_raw(WK, 0)
            for stage, arg in timeline:
                if stage == "idx":
                    if arg + 8 < U:
                        load_idx(arg + 8)
                    if arg:
                        store_idx(arg - 1)
                if stage == "gram" and arg % T == 2 and arg // T + 3 < NG:
                    load_gram(arg // T + 3)
                if stage == "raw":
                    if arg == (WO, 0):
                        store_idx(U - 1)
                    after = K * arg[0] + arg[1] + 1
                    load_raw(after // K, after % K)
            load_raw(WV, 1)
            load_raw(WV, 2)
            load_raw(WV, 3)

            def flat(tile):
                return tile[:].rearrange("p k d -> p (k d)").bitcast(F32)

            def load_x(b):
                sp.dma_start(x1[b.parity][:], xb_dram[b.n]).then_inc(x_loaded[b.parity], 16)

            def store(b):
                sp.wait_ge(y_added, b.count(T, T - 1))
                sp.dma_start(ob_dram[b.n], x1[b.parity][:]).then_inc(out_stored[b.parity], 16)

            def reload_x(b):
                sp.wait_ge(out_stored[b.parity], 16 * b.half)
                load_x(b)

            def load_m(b):
                sp.wait_ge(attn_done, T * b.n)
                for i, half in enumerate((m_hi, m_lo)):
                    sp.dma_start(flat(half), m_dram[b.half // (GB // 2), i]).then_inc(m_loaded, 16)

            sp.wait_ge(product_done, K * (number[(MIX, 1)] + 1))
            load_x(Block(0, 0))
            for b, pair in enumerate(((m_hi, m_lo), wa)):
                sp.wait_ge(product_lo, K * (number[(FOLD, b)] + 1))
                for i in range(2):
                    sp.dma_start(m_dram[b, i], flat(pair[i])).then_inc(m_stored, 16)
            sp.wait_ge(w_lo_done, U)
            load_x(Block(0, 1))
            sp.wait_ge(m_stored, 16 * 2 * B)
            store(Block(0, 0))
            reload_x(Block(0, 2))
            with sp.Fori(0, (NG - 4) // 2) as j:
                load_m(Block(j, 2))
                store(Block(j, 1))
                reload_x(Block(j, 3))
                store(Block(j, 2))
                reload_x(Block(j, 4))
            load_m(Block(0, NG - 2))
            store(Block(0, NG - 3))
            reload_x(Block(0, NG - 1))
            store(Block(0, NG - 2))
            store(Block(0, NG - 1))
            for i in range(2):
                sp.wait_ge(out_stored[i], 16 * (NG // 2))

        @blk.gpsimd
        def _(pool):
            pool.dma_start(lut[:], lut_in.rearrange("(a n) -> a n", a=1).to_broadcast([P, LUT])).then_inc(lut_loaded, 16)
            pool.memset(ident[:], 0.0).then_inc(const_made, 1)
            pool.memset(ident_bf[:], 0.0).then_inc(const_made, 1)
            for tile in idx_out:
                pool.memset(tile[:], 0).then_inc(idx_cleared, 1)
            pool.wait_ge(const_made, 2)
            for one in (ident, ident_bf):
                pool.affine_select(out=one[:], in_=one[:], compare_op=ALU.not_equal, fill=1.0, base=0,
                                   pattern=[[-1, P]], channel_multiplier=1).then_inc(const_made, 1)

            def low(out_, whole, high):
                return pool.tensor_tensor(out_, whole, high.bitcast(F32), ALU.subtract)

            def weight_low(u):
                c, kind = u // 3, u % 3
                pool.wait_ge(w_hi_done, u + 1)
                low(w_lo[c][:, kind, :], picked[u % 2][:], w_hi[c][:, kind, :]).then_inc(w_lo_done, 1)

            def make_leaves(k):
                if k == 0:
                    pool.wait_ge(step_made, 1)
                for u, j in leaves_at(k, POOL_LEAVES):
                    tile, high, step, entry = make_leaf(pool, u, j)
                    pool.tensor_scalar(tile, high, step, entry, ALU.mult, ALU.add).then_inc(pool_leaf_made, 1)

            for stage, arg in timeline:
                if stage == "gram_in":
                    i = arg
                    pool.wait_ge(xg_hi_done, i + 1)
                    low(xg_lo[i % 4][:], xg_n[i % 4][:], xg_hi[i % 4][:]).then_inc(xg_lo_done, 1)
                if stage == "raw":
                    w, k = arg
                    r = K * w + k
                    pool.wait_ge(raw_hi_done, r + 1)
                    hi, lo = split_into[w]
                    low(lo[:, k, :], raw[r % 2][:], hi[:, k, :]).then_inc(raw_lo_done, 1)
                if stage == "look":
                    make_leaves(arg)
                if stage == "built":
                    weight_low(arg)

            def build(looks):
                for k in looks:
                    make_leaves(k)
                    for u in built_by(k):
                        weight_low(u)

            def ffn(b):
                for c in range(C):
                    n = rows(c)
                    build(late_looks(b, c, 0))
                    pool.wait_ge(h_hi_done, b.count(C, c))
                    low(h_lo[c % 2][0:n, :], h_full[0:n, :], h_hi[c % 2][0:n, :]).then_inc(h_lo_done, 1)
                    build(late_looks(b, c, 1))

            ffn(Block(0, 0))
            every_block(pool, ffn)

        @blk.scalar
        def _(act):
            def fetch_idx(u):
                act.wait_ge(idx_stored[u % 4], 16 * (u // 4 + 1))
                act.dma_start(idx_in[u % 3][:], idx_dram[u]).then_inc(idx_back[u % 3], 16)

            def make_leaves(k):
                if k == 0:
                    act.wait_ge(step_made, 1)
                for u, j in leaves_at(k, LEAVES):
                    tile, high, step, entry = make_leaf(act, u, j)
                    act.activation(tile, high, ACT.Identity, bias=entry, scale=step).then_inc(leaf_made, 1)

            def weight_high(u):
                c, kind = u // 3, u % 3
                act.wait_ge(picked_done, u + 1)
                if u + 3 < U:
                    fetch_idx(u + 3)
                if u == 15:
                    act.wait_ge(product_done, K * (number[(MIX, 0)] + 1))
                if u == 18:
                    act.wait_ge(product_done, K * (number[(FOLD, 0)] + 1))
                if u == 24:
                    act.wait_ge(product_done, LAST_ITEM)
                if u == 30:
                    act.wait_ge(m_stored, 16 * 2 * B)
                act.copy(w_hi[c][:, kind, :], picked[u % 2][:]).then_inc(w_hi_done, 1)

            def turn_first(step):
                b = Block(0, 0)
                if step == "ln1":
                    for i in range(4):
                        act.wait_ge(idx_stored[i], 16 * ((U - 1 - i) // 4 + 1))
                    normalise(b, xn_first, 0)
                elif step == "ln2":
                    normalise(b, xn_first, 1)
                elif step == "x2":
                    x2_high(b)
                elif step[0] == "turn":
                    x_high(b, step[1])

            def normalise(b, into, second):
                scale, bias = rstd[second], shift[second]
                if second:
                    act.wait_ge(ln2_stats, b.count(1, 0))
                elif b.exposed:
                    act.wait_ge(x_loaded[b.parity], 16)
                    scale, bias = scale_of(b.n)
                else:
                    act.wait_ge(ln1_stats, b.n - 1)
                for t in range(T):
                    act.activation(into[:, t, :], x1[b.parity][:, t, :], ACT.Identity, bias=bias[:, t:t + 1],
                                   scale=scale[:, t:t + 1]).then_inc((ln1_done, ln2_done)[second], 1)

            def x_high(b, t):
                act.wait_ge(xt_turned, b.count(T, t))
                if b.between and t == 1:
                    act.wait_ge(h_lo_done, C)
                elif b.first and t == 0:
                    act.wait_ge(product_done, K * (number[(TURN_V, 0)] + 1))
                else:
                    act.wait_ge(attn_done, b.count(T, t - (2 if b.between and t else 1)))
                act.copy(xt_hi[b.xt(t)][:].rearrange("p k s -> p (k s)"), b.turn_bank(t)[:]).then_inc(xt_hi_done, 1)

            def x2_high(b):
                if b.first:
                    act.wait_ge(m_stored, 16 * 2 * B)
                for k in range(K):
                    act.wait_ge(x2_turned, b.count(K, k))
                    act.copy(x2t_hi[:, k, :], b.x2_bank(k)[:]).then_inc(x2_hi_done, 1)

            for stage, arg in timeline:
                if stage == "idx":
                    u, c, kind = arg, arg // 3, arg % 3
                    n = rows(c)
                    act.wait_ge(idx_turned, u + 1)
                    if u == 0:
                        act.wait_ge(idx_cleared, 4)
                    if u >= 4:
                        act.wait_ge(idx_stored[u % 4], 16 * (u // 4))
                    src = idx_bank(u)[:, 0:D].rearrange("p (k i) -> p k i", k=K)
                    dst = idx_out[u % 4][:].rearrange("p (k i) -> p k i", k=K)
                    if kind < 2:
                        src, dst = src[:, :, 0:n], dst[:, :, 0:n]
                    else:
                        src, dst = src[0:n], dst[0:n]
                    act.copy(dst, src).then_inc(idx_laid, 1)
                    if 4 <= u < 7:
                        fetch_idx(u - 4)
                if stage == "gram_n":
                    i = arg
                    g, t = i // T, i % T
                    act.wait_ge(xg_stats, g + 1)
                    if i >= 4:
                        act.wait_ge(xg_lo_done, i - 3)
                    scale, bias = scale_of(g)
                    act.activation(xg_n[i % 4][:], xg[g % 3][:, t, :], ACT.Identity, bias=bias[:, t:t + 1],
                                   scale=scale[:, t:t + 1]).then_inc(xg_normed, 1)
                if stage == "gram_in":
                    i = arg
                    act.wait_ge(xg_normed, i + 1)
                    if i >= 4:
                        act.wait_ge(xg_used, i - 3)
                    act.copy(xg_hi[i % 4][:], xg_n[i % 4][:]).then_inc(xg_hi_done, 1)
                if stage == "raw":
                    w, k = arg
                    r = K * w + k
                    act.wait_ge(raw_loaded[r % 2], 16 * (r // 2 + 1))
                    if w == WO:
                        act.wait_ge(product_done, K * (number[(PROD, 1)] + 1))
                    act.copy(split_into[w][0][:, k, :], raw[r % 2][:]).then_inc(raw_hi_done, 1)
                if stage == "take":
                    n = arg
                    hi, _ = result_of(n)
                    act.wait_ge(product_done, n + 1)
                    if is_score(n):
                        act.wait_ge(product_lo, n - 1)
                        s = n - K * number[(SCORE, 0)]
                        act.wait_ge(smax_done, s + 1)
                        act.mul(sbias[:, s:s + 1], smax[:, s:s + 1], -SCALE).then_inc(sbias_done, 1)
                        act.wait_ge(sbias_done, s + 1)
                        act.activation(full[n % 2][:], product_bank(n)[:], ACT.Exp, bias=sbias[:, s:s + 1], scale=SCALE,
                                       accum_out=ssum[:, s:s + 1]).then_inc(sexp_done, 1)
                    else:
                        if n == K * number[(FOLD, 1)]:
                            act.wait_ge(product_done, K * (number[(MIX, 1)] + 1))
                        act.copy(hi, as_result(n, product_bank(n))).then_inc(product_hi, 1)
                if stage == "norm":
                    n, s = arg, arg - K * number[(SCORE, 0)]
                    act.wait_ge(srec_done, s + 1)
                    act.activation(result_of(n)[0], full[n % 2][:], ACT.Copy, scale=srec[:, s:s + 1]).then_inc(product_hi, 1)
                if stage == "mirror":
                    (hi, lo), turned = mat_x[arg], bank[4 * arg:4 * arg + 3]
                    act.wait_ge(mirrored, arg + 1)
                    act.copy(hi[:, 2:K, 0:2 * P], turned[0][:].rearrange("p (k d) -> p k d", k=2))
                    act.copy(hi[:, 1, 0:P], turned[2][:, 0:P])
                    act.copy(lo[:, 1, 0:P], turned[2][:, P:2 * P]).then_inc(mirror_taken, 1)
                if stage == "look":
                    make_leaves(arg)
                if stage == "built":
                    weight_high(arg)
                if stage == "first":
                    turn_first(arg)

            def build(looks):
                for k in looks:
                    make_leaves(k)
                    for u in built_by(k):
                        weight_high(u)

            def ffn(b):
                for c in range(C):
                    n = rows(c)
                    act.wait_ge(gate_done, b.count(C, c))
                    if not (b.first and c == 0):
                        act.wait_ge(h_done, b.count(C, c - 1))
                    act.activation(h_gate[0:n, :], bank[4][0:n, :], ACT.Silu).then_inc(silu_done, 1)
                    build(late_looks(b, c, 0))
                    act.wait_ge(h_done, b.count(C, c))
                    if b.first and c == 0:
                        act.wait_ge(x2_turned, K)
                    if c >= 2:
                        act.wait_ge(down_done, b.count(C, c - 2))
                    elif not b.first:
                        act.wait_ge(down_done, b.count(C, -1))
                    act.copy(h_hi[c % 2][0:n, :], h_full[0:n, :]).then_inc(h_hi_done, 1)
                    build(late_looks(b, c, 1))
                    for step in preparation(b, c):
                        if step == "ln1":
                            act.wait_ge(x2_turned, b.count(K, K - 1))
                            normalise(b.next(), xn, 0)
                        elif step == "ln2":
                            act.wait_ge(xt_turned, b.next().count(T, T - 1))
                            normalise(b.next(), xn, 1)
                        elif step[0] == "turn":
                            x_high(b.next(), step[1])
                if not b.last:
                    x2_high(b.next())

            ffn(Block(0, 0))
            every_block(act, ffn)

        @blk.tensor
        def _(pe):
            def products(out_, terms):
                last = None
                for i, ((lh, ll), (rh, rl)) in enumerate(terms):
                    for j, (a, b) in enumerate(((lh, rh), (ll, rh), (lh, rl))):
                        last = pe.matmul(out_, a, b, start=(i == 0 and j == 0), stop=(i == len(terms) - 1 and j == 2))
                return last

            def turn_x(b, source, t):
                pe.wait_ge(ln1_done, b.count(T, t))
                if b.first and t == 0:
                    pe.wait_ge(product_lo, K * (number[(FOLD, 0)] + 1))
                elif t == 0:
                    pe.wait_ge(x2_lo_done, b.count(K, -1))
                elif b.between and t == 1:
                    pe.wait_ge(silu_done, C)
                else:
                    pe.wait_ge(xt_lo_done, b.count(T, t - (2 if b.between else 1)))
                for k in range(K):
                    last = pe.transpose(b.turn_bank(t)[:, k * P:(k + 1) * P], source[:, t, k * P:(k + 1) * P], ident[:])
                last.then_inc(xt_turned, 1)

            def attend(b, t):
                pe.wait_ge(xt_lo_done, b.count(T, t))
                if b.first and t == 0:
                    pe.wait_ge(product_lo, K * (number[(FOLD, 0)] + 1))
                if t:
                    pe.wait_ge(x1_done, b.count(T, t - 1))
                if not (isinstance(b.n, int) and b.n < 2):
                    pe.wait_ge(m_loaded, 32 * b.half)
                hi, lo = xt_hi[b.xt(t)], xt_lo[b.xt(t)]
                products(bank[7][:], [((hi[:, k, :], lo[:, k, :]), (m_hi[:, k, :], m_lo[:, k, :]))
                                      for k in range(K)]).then_inc(attn_done, 1)

            def turn_x2_by_tile(b, source):
                for t in range(T):
                    pe.wait_ge(ln2_done, b.count(T, t))
                    if b.between and t == 0:
                        pe.wait_ge(h_done, C)
                    for k in range(K):
                        last = pe.transpose(b.x2_bank(k)[:, t * P:(t + 1) * P], source[:, t, k * P:(k + 1) * P], ident[:])
                        if t == T - 1:
                            last.then_inc(x2_turned, 1)

            def turn_x2(b, source, k):
                if k == 0:
                    pe.wait_ge(ln2_done, b.count(T, T - 1))
                if k >= 2:
                    pe.wait_ge(x2_lo_done, b.count(K, k - 2))
                for t in range(T):
                    last = pe.transpose(bank[6 + k % 2][:, t * P:(t + 1) * P], source[:, t, k * P:(k + 1) * P], ident[:])
                last.then_inc(x2_turned, 1)

            operands = {PROD: (mat_x, wa), SCORE: (wb, mat_y), MIX: (mat_x, wa), FOLD: (wb, mat_y)}
            before = {PROD: GRAM, SCORE: PROD, MIX: SCORE, FOLD: MIX}
            weight = {PROD: WK, SCORE: WQ, MIX: WO}
            pe.wait_ge(const_made, 4)
            for stage, arg in timeline:
                if stage == "idx":
                    u, c, kind = arg, arg // 3, arg % 3
                    n = rows(c)
                    pe.wait_ge(idx_cast, u + 1)
                    if u >= 4:
                        pe.wait_ge(idx_laid, u - 3)
                    if u == U_HIGH_BANKS:
                        pe.wait_ge(product_lo, K)
                    if u == U_BEFORE_MIRROR:
                        pe.wait_ge(mirror_taken, 2)
                    turned = idx_bank(u)
                    for k in range(K):
                        if kind < 2:
                            last = pe.transpose(turned[:, k * P:k * P + n], idx_bf[u % 4][0:n, k * P:(k + 1) * P], ident_bf[0:n, 0:n])
                        else:
                            last = pe.transpose(turned[0:n, k * P:(k + 1) * P], idx_bf[u % 4][:, k * P:k * P + n], ident_bf[:])
                    last.then_inc(idx_turned, 1)
                if stage == "gram":
                    i, batch = arg, arg // (T * GB)
                    if i == T * GB:
                        pe.wait_ge(idx_laid, U_HIGH_BANKS)
                    pe.wait_ge(xg_lo_done, i + 1)
                    start, stop = i % (T * GB) == 0, i % (T * GB) == T * GB - 1
                    hi, lo = xg_hi[i % 4], xg_lo[i % 4]
                    for m in range(K):
                        rows_of, cols = slice(m * P, (m + 1) * P), slice(gram_first(m), D)
                        for j, (a, b) in enumerate(((hi, hi), (lo, hi), (hi, lo))):
                            last = pe.matmul(bank[4 * batch + m][:, cols], a[:, rows_of], b[:, cols],
                                             start=start and j == 0, stop=stop and j == 2)
                        if stop:
                            last.then_inc(product_done, 1)
                    if not stop:
                        last.then_inc(xg_used, 1)
                    elif i + 4 < T * NG:
                        pe.wait_ge(product_done, K * (batch + 1))
                        pe.sem_inc(xg_used, 1)
                if stage == "mirror":
                    b = arg
                    pe.wait_ge(product_lo, K * (b + 1))
                    if b == 0:
                        pe.wait_ge(idx_laid, U_BEFORE_MIRROR)
                    pairs = [(0, 2), (1, 2), (0, 3), (1, 3)]
                    for i, half in enumerate(mat_x[b]):
                        source = half[:].bitcast(F32)
                        for j, (row, col) in enumerate(pairs):
                            pe.transpose(bank[4 * b + i][:, j * P:(j + 1) * P], source[:, row, col * P:(col + 1) * P], ident[:])
                        last = pe.transpose(bank[4 * b + 2][:, i * P:(i + 1) * P], source[:, 0, P:2 * P], ident[:])
                    last.then_inc(mirrored, 1)
                if stage == "product":
                    n = arg
                    (name, b), m = groups[n // K], n % K
                    if name == PROD and m == 0:
                        pe.wait_ge(mirror_taken, 2 * (b + 1))
                        if b == 0:
                            pe.wait_ge(idx_laid, U)
                    pe.wait_ge(product_lo, n - 2 * K + 1)
                    if name == TURN_V:
                        r = K * WV + m
                        pe.wait_ge(raw_loaded[r % 2], 16 * (r // 2 + 1))
                        for k in range(K):
                            last = pe.transpose(product_bank(n)[:, k * P:(k + 1) * P], raw[r % 2][:, k * P:(k + 1) * P], ident[:])
                        last.then_inc(product_done, 1)
                        continue
                    left, right = operands[name]
                    left = left[b] if name in (PROD, MIX) else left
                    right = right if name in (PROD, MIX) else right[b]
                    pe.wait_ge(product_lo, K * (number[(before[name], b)] + 1))
                    if name in weight:
                        pe.wait_ge(raw_lo_done, K * (weight[name] + 1))
                    else:
                        pe.wait_ge(product_lo, K * (number[(TURN_V, 0)] + 1))
                    products(product_bank(n)[:], [([a[:, k, m * P:(m + 1) * P] for a in left], [a[:, k, :] for a in right])
                                                  for k in range(K)]).then_inc(product_done, 1)
                if stage == "first":
                    if arg == "x2":
                        turn_x2_by_tile(Block(0, 0), xn_first)
                    elif arg[0] == "turn":
                        turn_x(Block(0, 0), xn_first, arg[1])
                    elif arg[0] == "attend":
                        attend(Block(0, 0), arg[1])

            def ffn(b):
                def down(c):
                    n = rows(c)
                    pe.wait_ge(h_lo_done, b.count(C, c))
                    if c == 0 and not b.first:
                        pe.wait_ge(y_added, b.count(T, -1))
                    if b.first:
                        pe.wait_ge(w_lo_done, 3 * c + 3)
                        if c == 0:
                            pe.wait_ge(product_lo, LAST_ITEM)
                    for t in range(T):
                        tokens = slice(t * P, (t + 1) * P)
                        hi, lo = h_hi[c % 2][0:n, tokens], h_lo[c % 2][0:n, tokens]
                        w = w_hi[c][0:n, 2, :], w_lo[c][0:n, 2, :]
                        for j, (a, x) in enumerate(((hi, w[0]), (lo, w[0]), (hi, w[1]))):
                            last = pe.matmul(bank[t][:], a, x, start=(c == 0 and j == 0), stop=(c == C - 1 and j == 2))
                    last.then_inc(down_done, 1)

                for c in range(C):
                    n = rows(c)
                    if c == 0:
                        pe.wait_ge(x2_lo_done, b.count(K, K - 1))
                    for kind, done, read in ((0, gate_done, silu_done), (1, up_done, h_done)):
                        if b.first:
                            pe.wait_ge(w_lo_done, 3 * c + kind + 1)
                        if not (b.first and c == 0):
                            pe.wait_ge(read, b.count(C, c - 1))
                        products(bank[4 + kind][0:n, :],
                                 [([w[c][:, kind, k * P:k * P + n] for w in (w_hi, w_lo)], (x2t_hi[:, k, :], x2t_lo[:, k, :]))
                                  for k in range(K)]).then_inc(done, 1)
                    for step in preparation(b, c):
                        if step[0] == "turn":
                            turn_x(b.next(), xn, step[1])
                        elif step[0] == "attend":
                            attend(b.next(), step[1])
                        elif step == "down":
                            down(c - 1)
                        elif step == "last down":
                            down(c)
                    if b.first and c == C - 1:
                        turn_x2_by_tile(b.next(), xn)
                    elif c == C - 1 and not b.last:
                        turn_x2(b.next(), xn, 0)
                        turn_x2(b.next(), xn, 1)
                    if c and not (b.first and c == C - 1):
                        down(c - 1)
                if not b.first:
                    if not b.last:
                        turn_x2(b.next(), xn, 2)
                        turn_x2(b.next(), xn, 3)
                    down(C - 1)

            ffn(Block(0, 0))
            every_block(pe, ffn)

        @blk.vector
        def _(dve):
            class Steps:
                base, n = 0, 0

            def step(ins):
                Steps.n += 1
                ins.then_inc(dve_steps, 1)
                return Steps.base + Steps.n

            def need(value):
                dve.wait_ge(dve_steps, value)

            def norm_stats(x, scale, bias, done, tiles=range(T)):
                for t in tiles:
                    last = dve.bn_stats(bn[:, t, :], x[:, t, :])
                last = step(last)
                yield
                need(last)
                dve.memset(tmp[:], 0.0)
                for t in range(T):
                    last = dve.bn_aggr(mv[:, t, :], bn[:, t, :])
                last = step(last)
                yield
                need(last)
                last = step(dve.tensor_scalar(var[:], mv[:, :, 1], EPS, None, ALU.add))
                yield
                need(last)
                y = scale
                last = step(dve.tensor_scalar(y[:].bitcast(I32), var[:].bitcast(I32), -0.5, RSQRT_SEED, ALU.mult, ALU.add))
                yield
                for _ in range(NEWTON):
                    need(last)
                    last = step(dve.tensor_tensor(tmp[:], y[:], y[:], ALU.mult))
                    yield
                    need(last)
                    last = step(dve.scalar_tensor_tensor(out=tmp[:], in0=tmp[:], scalar=-0.5, in1=var[:], op0=ALU.mult, op1=ALU.mult))
                    yield
                    need(last)
                    last = step(dve.scalar_tensor_tensor(out=y[:], in0=tmp[:], scalar=1.5, in1=y[:], op0=ALU.add, op1=ALU.mult))
                    yield
                need(last)
                dve.scalar_tensor_tensor(out=bias[:], in0=mv[:, :, 0], scalar=-1.0, in1=y[:], op0=ALU.mult,
                                         op1=ALU.mult).then_inc(done, 1)
                yield

            STEPS_PER_NORM = NORM_PIECES - 1

            def merge(bit, keep, other):
                return dve.copy_predicated(keep[:], bit_mask[bit][:], other[:])

            def pairs_of(byte):
                return byte * 257

            def find_bit(u, bit):
                return step(dve.tensor_scalar(bit_mask[bit][:].bitcast(I16), idx_in[u % 3][:].bitcast(I16), pairs_of(1 << bit),
                                              None, ALU.bitwise_and))

            def find_high(u):
                dve.wait_ge(idx_back[u % 3], 16 * (u // 3 + 1))
                if u >= 2:
                    dve.wait_ge(leaf_made, leaf_count(u - 2, 6))
                dve.tensor_scalar(high_bit[u % 2][:].bitcast(I16), idx_in[u % 3][:].bitcast(I16), HIGH_BIT, pairs_of(1),
                                  ALU.logical_shift_right, ALU.bitwise_and).then_inc(high_made, 1)

            def look_up():
                x, y, z, w, v = part
                find_high(0)
                for bit in range(3):
                    ready = find_bit(0, bit)
                for u in range(U):
                    r, more = picked[u % 2], u + 1 < U
                    need(ready)
                    dve.wait_ge(leaf_made, leaf_count(u, 3))
                    merge(0, y, z).then_inc(merged, 1)
                    yield
                    dve.wait_ge(leaf_made, leaf_count(u, 1))
                    dve.wait_ge(pool_leaf_made, pool_leaf_count(u, 0))
                    merge(0, r, x).then_inc(merged, 1)
                    yield
                    dve.wait_ge(pool_leaf_made, pool_leaf_count(u, 4))
                    merge(0, w, v).then_inc(merged, 1)
                    yield
                    dve.wait_ge(merged, merge_count(u, M_RX))
                    merge(1, r, y).then_inc(merged, 1)
                    yield
                    if more:
                        find_high(u + 1)
                    yield
                    dve.wait_ge(leaf_made, leaf_count(u, 6))
                    merge(0, x, z).then_inc(merged, 1)
                    yield
                    dve.wait_ge(merged, merge_count(u, M_XZ))
                    merge(1, w, x).then_inc(merged, 1)
                    yield
                    if more:
                        find_bit(u + 1, 0)
                    yield
                    dve.wait_ge(merged, merge_count(u, M_WX))
                    merge(2, r, w).then_inc(picked_done, 1)
                    yield
                    if more:
                        find_bit(u + 1, 1)
                    yield
                    if more:
                        dve.wait_ge(picked_done, u + 1)
                        ready = find_bit(u + 1, 2)
                    yield

            def x_low(b, t):
                dve.wait_ge(xt_hi_done, b.count(T, t))
                hi, lo = (a[b.xt(t)][:].rearrange("p k s -> p (k s)") for a in (xt_hi, xt_lo))
                dve.tensor_tensor(lo, b.turn_bank(t)[:], hi.bitcast(F32), ALU.subtract).then_inc(xt_lo_done, 1)

            def add_attention(b, t):
                dve.wait_ge(attn_done, b.count(T, t))
                dve.wait_ge(ln1_done, b.count(T, t))
                dve.tensor_tensor(x1[b.parity][:, t, :], bank[7][:], x1[b.parity][:, t, :], ALU.add).then_inc(x1_done, 1)
                if t:
                    dve.wait_ge(x1_done, b.count(T, t - 1))
                    dve.bn_stats(bn[:, t - 1, :], x1[b.parity][:, t - 1, :])

            def x2_low(b):
                for k in range(K):
                    dve.wait_ge(x2_hi_done, b.count(K, k))
                    dve.tensor_tensor(x2t_lo[:, k, :], b.x2_bank(k)[:], x2t_hi[:, k, :].bitcast(F32),
                                      ALU.subtract).then_inc(x2_lo_done, 1)

            def stats1(b):
                dve.wait_ge(x_loaded[b.parity], 16 * (b.half + 1))
                dve.wait_ge(ln1_done, b.count(T, -1))
                return norm_stats(x1[b.parity], rstd[0], shift[0], ln1_stats)

            def stats2(b):
                dve.wait_ge(x1_done, b.count(T, T - 1))
                if not b.first:
                    dve.wait_ge(ln2_done, b.count(T, -1))
                return norm_stats(x1[b.parity], rstd[1], shift[1], ln2_stats, [T - 1])

            first = Block(0, 0)
            looks = look_up()
            dve.wait_ge(lut_loaded, 16)
            dve.tensor_tensor(lut_step[:], lut[:, HALF:LUT], lut[:, 0:HALF], ALU.subtract).then_inc(step_made, 1)
            dve.wait_ge(step_made, 1)
            for stage, arg in timeline:
                if stage == "cast":
                    u, c, kind = arg, arg // 3, arg % 3
                    n = rows(c)
                    dve.wait_ge(idx_loaded[u % 8], 16 * (u // 8 + 1))
                    if u >= 4:
                        dve.wait_ge(idx_turned, u - 3)
                    src, dst = idx_raw[u % 8][:, :], idx_bf[u % 4][:, :]
                    if kind < 2:
                        src, dst = src[0:n, :], dst[0:n, :]
                    else:
                        src, dst = (a.rearrange("p (k i) -> p k i", k=K)[:, :, 0:n] for a in (src, dst))
                    dve.tensor_copy(dst, src).then_inc(idx_cast, 1)
                if stage == "stats":
                    g = arg
                    dve.wait_ge(xg_loaded[g % 3], 16 * (g // 3 + 1))
                    if g >= 4:
                        dve.wait_ge(xg_normed, T * (g - 1))
                    stats = norm_stats(xg[g % 3], *scale_of(g), xg_stats)
                    next(stats)
                if stage == "stats_go_on":
                    next(stats)
                if stage == "take" and not is_score(arg):
                    hi, lo = result_of(arg)
                    dve.wait_ge(product_hi, arg + 1)
                    dve.tensor_tensor(lo, as_result(arg, product_bank(arg)), hi.bitcast(F32), ALU.subtract).then_inc(product_lo, 1)
                if stage == "mirror":
                    lo, turned = mat_x[arg][1], bank[4 * arg:4 * arg + 3]
                    dve.wait_ge(mirrored, arg + 1)
                    dve.tensor_copy(lo[:, 2:K, 0:2 * P], turned[1][:].rearrange("p (k d) -> p k d", k=2)).then_inc(mirror_taken, 1)
                if stage == "take" and is_score(arg):
                    s = arg - K * number[(SCORE, 0)]
                    dve.wait_ge(product_done, arg + 1)
                    dve.reduce_max(smax[:, s:s + 1], product_bank(arg)[:], AX_X).then_inc(smax_done, 1)
                if stage == "norm":
                    s = arg - K * number[(SCORE, 0)]
                    dve.wait_ge(sexp_done, s + 1)
                    dve.reciprocal(srec[:, s:s + 1], ssum[:, s:s + 1]).then_inc(srec_done, 1)
                if stage == "norm_low":
                    s = arg - K * number[(SCORE, 0)]
                    hi, lo = result_of(arg)
                    dve.wait_ge(srec_done, s + 1)
                    dve.wait_ge(product_hi, arg + 1)
                    dve.scalar_tensor_tensor(out=lo, in0=full[arg % 2][:], scalar=srec[:, s:s + 1], in1=hi.bitcast(F32),
                                             op0=ALU.mult, op1=ALU.subtract).then_inc(product_lo, 1)
                if stage == "look":
                    next(looks)
                if stage == "first":
                    if arg == "stats2":
                        dve.wait_ge(xg_normed, T * NG)
                        stats = stats2(first)
                        next(stats)
                    elif arg == "x2":
                        x2_low(first)
                    elif arg[0] == "turn":
                        x_low(first, arg[1])
                    elif arg[0] == "attend":
                        add_attention(first, arg[1])

            def ffn(b):
                for c in range(C):
                    n = rows(c)
                    for _ in late_looks(b, c, 0):
                        next(looks)
                    dve.wait_ge(up_done, b.count(C, c))
                    dve.wait_ge(silu_done, b.count(C, c))
                    if not (b.first and c == 0):
                        dve.wait_ge(h_lo_done, b.count(C, c - 1))
                    dve.tensor_tensor(h_full[0:n, :], bank[5][0:n, :], h_gate[0:n, :], ALU.mult).then_inc(h_done, 1)
                    for _ in late_looks(b, c, 1):
                        next(looks)
                    for s in preparation(b, c):
                        if s == "stats1":
                            list(stats1(b.next()))
                        elif s == "stats2":
                            list(stats2(b.next()))
                        elif s[0] == "turn":
                            x_low(b.next(), s[1])
                        elif s[0] == "attend":
                            add_attention(b.next(), s[1])
                if not b.last:
                    x2_low(b.next())
                dve.wait_ge(down_done, b.count(C, C - 1))
                for t in range(T):
                    dve.tensor_tensor(x1[b.parity][:, t, :], bank[t][:], x1[b.parity][:, t, :], ALU.add).then_inc(y_added, 1)

            ffn(first)
            begun, pairs = Steps.n, (NG - 2) // 2
            with dve.Fori(0, pairs) as j:
                Steps.base, Steps.n = 4 * STEPS_PER_NORM * j, begun
                ffn(Block(j, 1))
                ffn(Block(j, 2))
            assert Steps.n == begun + 4 * STEPS_PER_NORM
            Steps.base, Steps.n = 0, begun + 4 * STEPS_PER_NORM * pairs
            ffn(Block(0, NG - 1))


_INS = ["L0_attn_x", "L0_attn_Wq", "L0_attn_Wk", "L0_attn_Wv", "L0_attn_Wo", "L0_ffn_lut", "L0_ffn_gate_idx",
        "L0_ffn_up_idx", "L0_ffn_down_idx"]
_ARGS = ["x_in", "wq_in", "wk_in", "wv_in", "wo_in", "lut_in", "gate_in", "up_in", "down_in"]


def kernel(**inputs):
    import numpy as _np
    import concourse.bacc as _bacc
    from concourse import mybir as _mybir
    from concourse.bass_utils import run_bass_kernel_spmd as _run

    nc = _bacc.Bacc("TRN2", target_bir_lowering=False, num_devices=1)
    arrays, args = {}, {}
    for name, arg in zip(_INS, _ARGS):
        a = _np.ascontiguousarray(inputs[name])
        arrays[f"in_{name}"] = a
        args[arg] = nc.dram_tensor(f"in_{name}", a.shape, _mybir.dt.from_np(a.dtype), kind="ExternalInput").ap()
    shape = arrays["in_L0_attn_x"].shape
    out = nc.dram_tensor("out_dram", shape, _mybir.dt.float32, kind="ExternalOutput").ap()
    preln_attention_ghost_ffn(nc, out=out, **args)
    r = _run(nc, [arrays], core_ids=[0])
    return r.results[0]["out_dram"]
```
